# Optimizing a Trainium2 kernel written in Bass

```python
import numpy as np
import jax
import jax.numpy as jnp

def _softmax(x, axis=-1):
    return jax.nn.softmax(x, axis=axis)

def _gelu(x):
    return jax.nn.gelu(x, approximate=True)

def _silu(x):
    return jax.nn.silu(x)

def _sigmoid(x):
    return jax.nn.sigmoid(x)

def _layernorm(x, axis=-1, eps=1e-05):
    m = jnp.mean(x, axis=axis, keepdims=True)
    v = jnp.var(x, axis=axis, keepdims=True)
    return (x - m) / jnp.sqrt(v + eps)

def _scatter_add(tgt, idx, src, axis=0):
    return tgt.at[idx].add(src)

def _segment_sum(src, seg, n):
    return jax.ops.segment_sum(src, seg, n)
kernel_name = 'mk_macaron_d2_jaxref_r8_ce9458'

def setup_inputs(seed: int=0):
    np.random.seed(seed)
    _w = jnp.asarray

    def _L0_attn_setup():
        import jax, jax.numpy as jnp
        import numpy as np
        import math
        D_MODEL = 512
        NUM_HEADS = 32
        NUM_KV_HEADS = 8
        HEAD_DIM = D_MODEL // NUM_HEADS
        GROUP = NUM_HEADS // NUM_KV_HEADS
        SEQ_LEN = 256
        BATCH = 2
        ROPE_THETA = 10000.0

        def apply_rope(x, start_pos=0):
            b, h, s, hd = x.shape
            inv_freq = 1.0 / ROPE_THETA ** (jnp.arange(0, hd, 2, dtype=jnp.float32) / hd)
            pos = jnp.arange(start_pos, start_pos + s, dtype=jnp.float32)
            ang = pos[:, None] * inv_freq[None, :]
            cos = jnp.cos(ang).astype(x.dtype)
            sin = jnp.sin(ang).astype(x.dtype)
            xr = x[..., 0::2]
            xi = x[..., 1::2]
            out_r = xr * cos - xi * sin
            out_i = xr * sin + xi * cos
            return jnp.stack([out_r, out_i], axis=-1).reshape(b, h, s, hd)
        key = jax.random.key(seed)
        ks = jax.random.split(key, 5)
        qkv_dim = HEAD_DIM * (NUM_HEADS + 2 * NUM_KV_HEADS)
        scale = 1.0 / math.sqrt(D_MODEL)
        return {'x': jax.random.normal(ks[0], (BATCH, SEQ_LEN, D_MODEL), jnp.float32), 'w_qkv': jax.random.normal(ks[1], (qkv_dim, D_MODEL), jnp.float32) * scale, 'b_qkv': jax.random.normal(ks[2], (qkv_dim,), jnp.float32) * 0.01, 'w_o': jax.random.normal(ks[3], (D_MODEL, D_MODEL), jnp.float32) * scale, 'b_o': jax.random.normal(ks[4], (D_MODEL,), jnp.float32) * 0.01}
    _L0_attn_in = _L0_attn_setup()

    def _L0_ffn_setup():
        import jax, jax.numpy as jnp
        import numpy as np
        B, S, DIN, DOUT, R = (2, 256, 512, 512, 32)
        key = jax.random.key(seed)
        k1, k2, k3, k4, k5 = jax.random.split(key, 5)
        std = 1.0 / np.sqrt(R)
        return {'x': jax.random.normal(k1, (B, S, DIN), dtype=jnp.float32), 'W': jax.random.normal(k2, (DOUT, DIN), dtype=jnp.float32) * 0.02, 'lora_A': jax.random.normal(k3, (R, DIN), dtype=jnp.float32) * std, 'lora_B': jax.random.normal(k4, (DOUT, R), dtype=jnp.float32) * 0.01, 'magnitude': jax.random.uniform(k5, (DOUT,), dtype=jnp.float32) + 0.5}
    _L0_ffn_in = _L0_ffn_setup()

    def _L1_attn_setup():
        import jax, jax.numpy as jnp
        import numpy as np
        B, S, HIDDEN = (2, 256, 512)
        TP = 2
        PART = HIDDEN // TP
        NUM_HEADS = 16 // TP
        HEAD_DIM = PART // NUM_HEADS
        MASKED_BIAS = -10000.0
        key = jax.random.key(seed)
        k_x, k_wq, k_bq, k_wo, k_bo = jax.random.split(key, 5)
        x = jax.random.normal(k_x, (B, S, HIDDEN), dtype=jnp.float32)
        w_qkv = jax.random.normal(k_wq, (3 * PART, HIDDEN), dtype=jnp.float32) * 0.02
        b_qkv = jax.random.normal(k_bq, (3 * PART,), dtype=jnp.float32) * 0.02
        w_o = jax.random.normal(k_wo, (HIDDEN, PART), dtype=jnp.float32) * 0.02
        b_o = jax.random.normal(k_bo, (HIDDEN,), dtype=jnp.float32) * 0.02
        return {'x': x, 'w_qkv': w_qkv, 'b_qkv': b_qkv, 'w_o': w_o, 'b_o': b_o}
    _L1_attn_in = _L1_attn_setup()

    def _L1_ffn_setup():
        import jax, jax.numpy as jnp
        import numpy as np
        B, S, D, O, E, R = (2, 512, 512, 512, 8, 16)
        TOP_K = 2
        SCALING = 32.0 / 16.0
        key = jax.random.key(seed)
        k = jax.random.split(key, 6)
        x = jax.random.normal(k[0], (B, S, D), dtype=jnp.float32)
        W_base = jax.random.normal(k[1], (O, D), dtype=jnp.float32) * 0.02
        b_base = jax.random.normal(k[2], (O,), dtype=jnp.float32) * 0.02
        W_router = jax.random.normal(k[3], (E, D), dtype=jnp.float32) * 0.01
        lora_A = jax.random.normal(k[4], (E, R, D), dtype=jnp.float32) * (1.0 / np.sqrt(D))
        lora_B = jax.random.normal(k[5], (E, O, R), dtype=jnp.float32) * 0.02
        return {'x': x, 'W_base': W_base, 'b_base': b_base, 'W_router': W_router, 'lora_A': lora_A, 'lora_B': lora_B}
    _L1_ffn_in = _L1_ffn_setup()
    _d = {'L0_attn_x': _L0_attn_in['x'], 'L0_attn_w_qkv': _L0_attn_in['w_qkv'], 'L0_attn_b_qkv': _L0_attn_in['b_qkv'], 'L0_attn_w_o': _L0_attn_in['w_o'], 'L0_attn_b_o': _L0_attn_in['b_o'], 'L0_ffn_W': _L0_ffn_in['W'], 'L0_ffn_lora_A': _L0_ffn_in['lora_A'], 'L0_ffn_lora_B': _L0_ffn_in['lora_B'], 'L0_ffn_magnitude': _L0_ffn_in['magnitude'], 'L1_attn_w_qkv': _L1_attn_in['w_qkv'], 'L1_attn_b_qkv': _L1_attn_in['b_qkv'], 'L1_attn_w_o': _L1_attn_in['w_o'], 'L1_attn_b_o': _L1_attn_in['b_o'], 'L1_ffn_W_base': _L1_ffn_in['W_base'], 'L1_ffn_b_base': _L1_ffn_in['b_base'], 'L1_ffn_W_router': _L1_ffn_in['W_router'], 'L1_ffn_lora_A': _L1_ffn_in['lora_A'], 'L1_ffn_lora_B': _L1_ffn_in['lora_B']}
    _x0 = _d['L0_attn_x']
    _d['L0_attn_x'] = jax.random.normal(jax.random.fold_in(jax.random.key(seed), 1), (2, 1024, 512), dtype=_x0.dtype)
    del _x0
    return _d

def reference(L0_attn_x, L0_attn_w_qkv, L0_attn_b_qkv, L0_attn_w_o, L0_attn_b_o, L0_ffn_W, L0_ffn_lora_A, L0_ffn_lora_B, L0_ffn_magnitude, L1_attn_w_qkv, L1_attn_b_qkv, L1_attn_w_o, L1_attn_b_o, L1_ffn_W_base, L1_ffn_b_base, L1_ffn_W_router, L1_ffn_lora_A, L1_ffn_lora_B):

    def _L0_attn_ref(x, w_qkv, b_qkv, w_o, b_o):
        import jax, jax.numpy as jnp
        import numpy as np
        import math
        D_MODEL = 512
        NUM_HEADS = 32
        NUM_KV_HEADS = 8
        HEAD_DIM = D_MODEL // NUM_HEADS
        GROUP = NUM_HEADS // NUM_KV_HEADS
        SEQ_LEN = 256
        BATCH = 2
        ROPE_THETA = 10000.0

        def apply_rope(x, start_pos=0):
            b, h, s, hd = x.shape
            inv_freq = 1.0 / ROPE_THETA ** (jnp.arange(0, hd, 2, dtype=jnp.float32) / hd)
            pos = jnp.arange(start_pos, start_pos + s, dtype=jnp.float32)
            ang = pos[:, None] * inv_freq[None, :]
            cos = jnp.cos(ang).astype(x.dtype)
            sin = jnp.sin(ang).astype(x.dtype)
            xr = x[..., 0::2]
            xi = x[..., 1::2]
            out_r = xr * cos - xi * sin
            out_i = xr * sin + xi * cos
            return jnp.stack([out_r, out_i], axis=-1).reshape(b, h, s, hd)
        bs, seq_len, d_model = x.shape
        qkv = x @ w_qkv.T + b_qkv
        q_dim = NUM_HEADS * HEAD_DIM
        kv_dim = NUM_KV_HEADS * HEAD_DIM
        q, k, v = jnp.split(qkv, [q_dim, q_dim + kv_dim], axis=-1)
        q = q.reshape(bs, seq_len, NUM_HEADS, HEAD_DIM).transpose(0, 2, 1, 3)
        k = k.reshape(bs, seq_len, NUM_KV_HEADS, HEAD_DIM).transpose(0, 2, 1, 3)
        v = v.reshape(bs, seq_len, NUM_KV_HEADS, HEAD_DIM).transpose(0, 2, 1, 3)
        q = apply_rope(q, 0)
        k = apply_rope(k, 0)
        k = jnp.repeat(k, GROUP, axis=1)
        v = jnp.repeat(v, GROUP, axis=1)
        scores = jnp.einsum('bhqd,bhkd->bhqk', q, k) / math.sqrt(HEAD_DIM)
        causal = jnp.tril(jnp.ones((seq_len, seq_len), dtype=bool))
        scores = jnp.where(causal[None, None, :, :], scores, jnp.float32(-1e+20))
        attn = jax.nn.softmax(scores, axis=-1)
        out = jnp.einsum('bhqk,bhkd->bhqd', attn, v)
        out = out.transpose(0, 2, 1, 3).reshape(bs, seq_len, d_model)
        return out @ w_o.T + b_o

    def _L0_ffn_ref(x, W, lora_A, lora_B, magnitude):
        import jax, jax.numpy as jnp
        import numpy as np
        B, S, DIN, DOUT, R = (2, 256, 512, 512, 32)
        base = jnp.einsum('bsi,oi->bso', x, W)
        lora = jnp.einsum('bsr,or->bso', jnp.einsum('bsi,ri->bsr', x, lora_A), lora_B)
        eff_W = W + lora_B @ lora_A
        column_norm = jax.lax.stop_gradient(jnp.sqrt(jnp.sum(eff_W * eff_W, axis=1)))
        result = (base + lora) / column_norm[None, None, :]
        return result * magnitude[None, None, :]

    def _L1_attn_ref(x, w_qkv, b_qkv, w_o, b_o):
        import jax, jax.numpy as jnp
        import numpy as np
        B, S, HIDDEN = (2, 256, 512)
        TP = 2
        PART = HIDDEN // TP
        NUM_HEADS = 16 // TP
        HEAD_DIM = PART // NUM_HEADS
        MASKED_BIAS = -10000.0
        b, s, _ = x.shape
        qkv = x @ w_qkv.T + b_qkv
        q, k, v = jnp.split(qkv, 3, axis=-1)

        def to_heads(a):
            return a.reshape(b, s, NUM_HEADS, HEAD_DIM).transpose(0, 2, 1, 3)
        q, k, v = (to_heads(q), to_heads(k), to_heads(v))
        scores = jnp.einsum('bhfc,bhtc->bhft', k, q)
        causal = jnp.triu(jnp.ones((s, s), dtype=bool))
        scores = jnp.where(causal[None, None], scores, MASKED_BIAS)
        attn = jax.nn.softmax(scores, axis=-2)
        vals = jnp.einsum('bhft,bhfc->bhtc', attn, v)
        vals = vals.transpose(0, 2, 1, 3).reshape(b, s, PART)
        out = vals @ w_o.T + b_o
        return out

    def _L1_ffn_ref(x, W_base, b_base, W_router, lora_A, lora_B):
        import jax, jax.numpy as jnp
        import numpy as np
        B, S, D, O, E, R = (2, 512, 512, 512, 8, 16)
        TOP_K = 2
        SCALING = 32.0 / 16.0
        d = x.shape[-1]
        n_experts = W_router.shape[0]
        xf = x.reshape(-1, d)
        logits = xf @ W_router.T
        probs = jax.nn.softmax(logits, axis=-1)
        topk_p, topk_i = jax.lax.top_k(probs, TOP_K)
        topk_p = topk_p / jnp.sum(topk_p, axis=-1, keepdims=True)
        w = jnp.sum(jax.nn.one_hot(topk_i, n_experts, dtype=xf.dtype) * topk_p[..., None], axis=1)
        h = jnp.einsum('td,erd->ter', xf, lora_A)
        lora_out = jnp.einsum('ter,eor,te->to', h, lora_B, w) * SCALING
        base = x @ W_base.T + b_base
        return base + lora_out.reshape(x.shape[:-1] + (W_base.shape[0],))
    x = L0_attn_x
    x = x + 0.5 * _L0_ffn_ref(_layernorm(x, axis=-1), L0_ffn_W, L0_ffn_lora_A, L0_ffn_lora_B, L0_ffn_magnitude)
    x = x + _L0_attn_ref(_layernorm(x, axis=-1), L0_attn_w_qkv, L0_attn_b_qkv, L0_attn_w_o, L0_attn_b_o)
    x = x + 0.5 * _L0_ffn_ref(_layernorm(x, axis=-1), L0_ffn_W, L0_ffn_lora_A, L0_ffn_lora_B, L0_ffn_magnitude)
    x = x + 0.5 * _L1_ffn_ref(_layernorm(x, axis=-1), L1_ffn_W_base, L1_ffn_b_base, L1_ffn_W_router, L1_ffn_lora_A, L1_ffn_lora_B)
    x = x + _L1_attn_ref(_layernorm(x, axis=-1), L1_attn_w_qkv, L1_attn_b_qkv, L1_attn_w_o, L1_attn_b_o)
    x = x + 0.5 * _L1_ffn_ref(_layernorm(x, axis=-1), L1_ffn_W_base, L1_ffn_b_base, L1_ffn_W_router, L1_ffn_lora_A, L1_ffn_lora_B)
    return x

_drawn_inputs = setup_inputs


def setup_inputs(seed=0):
    import zlib

    import numpy as np

    out = dict(_drawn_inputs(seed))
    spreads = {}
    factors = {'L0_attn_b_qkv': 6.431,
     'L0_attn_b_o': 7.253,
     'L1_attn_w_qkv': 3.148,
     'L1_attn_b_qkv': 8.0,
     'L1_attn_b_o': 4.889,
     'L1_ffn_b_base': 5.083}
    for name, (base, spread) in spreads.items():
        noise = np.random.default_rng([zlib.crc32(name.encode()), seed]).standard_normal(out[name].shape)
        drawn = base * np.exp(spread * noise) if base else spread * noise
        out[name] = jnp.asarray(drawn.astype(out[name].dtype))
    for name, factor in factors.items():
        out[name] = (out[name] * factor).astype(out[name].dtype)
    return out
```

```python
from contextlib import ExitStack

import numpy as np

import concourse.bass as bass
from concourse import mybir

F32 = mybir.dt.float32
BF16 = mybir.dt.bfloat16
U32 = mybir.dt.uint32
ALU = mybir.AluOpType
ACT = mybir.ActivationFunctionType
AX = mybir.AxisListType

P = 128
BATCH, SEQ, D = 2, 1024, 512
NT = SEQ // P
KC = D // P
HALF = 512
EPS = 1e-5
EXPERTS, RANK = 8, 16
ER = EXPERTS * RANK
NEG = -1e30
AHEAD = 1.2


class Attention:

    def __init__(self, name, q_heads, kv_heads, dim, scale, unit_heads, rope):
        self.name, self.dim, self.scale, self.rope = name, dim, scale, rope
        self.unit_heads = unit_heads
        self.units = q_heads // unit_heads
        self.kv_heads = kv_heads
        self.grouped = q_heads != kv_heads
        self.q_feats, self.kv_feats = q_heads * dim, kv_heads * dim
        self.qk_feats = self.q_feats + self.kv_feats
        self.feats = self.qk_feats + self.kv_feats
        self.blocks = self.qk_feats // P
        self.rows = P // unit_heads
        self.k_copies = 1 if self.grouped else unit_heads
        self.pairs = unit_heads // 2
        self.lag = 2 if self.pairs == 2 else 3
        self.chunks = 2 * self.units
        self.steps = [(c, j, max(HALF * c, P * j), HALF * (c + 1) - max(HALF * c, P * j))
                      for c in range(2) for j in range(4 * c + 4)]
        self.last_step = [3, len(self.steps) - 1]
        six = [(1, 1), (1, 2), (2, 1), (2, 2), (1, 3), (3, 1)]
        self.main_parts = six if dim == 16 else six[:3]
        self.rest_parts = [] if dim == 16 else six[3:]
        self.main_loads, self.rest_loads = self.loads(self.main_parts), self.loads(self.rest_parts)
        self.max_chunks = []
        for t in range(NT):
            for kp in range(1 + (t >= 4)):
                w = P * (t + 1) - HALF * kp if kp or t < 4 else HALF
                n = min(HALF // w, unit_heads)
                self.max_chunks += [(t, kp, w, h, n) for h in range(0, unit_heads, n)]
        self.slots = 3
        self.plan_ring()

    def loads(self, rows):
        nq, nk = self.unit_heads, self.k_copies
        out = []
        for i, (pq, pk) in enumerate(rows):
            out += [(i, pq, 0, nq + nk)] if pq == pk else [(i, pq, 0, nq), (i, pk, nq, nk)]
        return out

    def feature_order(self):
        def blocks(first, heads):
            f = first + np.arange(heads * self.units * self.dim).reshape(self.units, heads, self.dim)
            return f.transpose(1, 0, 2).reshape(-1)
        return np.concatenate([blocks(0, self.unit_heads), blocks(self.q_feats, self.k_copies),
                               np.arange(self.qk_feats, self.feats)])

    def plan_ring(self):
        ns = len(self.steps)
        total = self.units * ns
        chunks = [(u, n) for u in range(self.units) for n in range(len(self.max_chunks))]
        per = len(self.max_chunks)
        ahead = int(per * AHEAD)
        self.ring_at = [[[] for _ in range(self.slots)] for _ in range(total + self.lag + 4)]
        self.ring_first = []
        width = [s[3] for s in self.steps]
        done, due_m = 0, []

        def push(dst, upto):
            nonlocal done
            while done < min(upto, len(chunks)):
                u, n = chunks[done]
                dst.append(("max", u, n))
                for x in due_m:
                    x[1] -= 1
                while due_m and due_m[0][1] <= 0:
                    dst.append(("shift", due_m.pop(0)[0], 0))
                if n == per - 1:
                    due_m.append([u, 3])
                done += 1

        push(self.ring_first, ahead)
        for s in range(total + self.lag + 4):
            for slot in range(self.slots):
                dst = self.ring_at[s][slot]
                if s < total:
                    u, k = divmod(s, ns)
                    share = (sum(width[:k]) + width[k] * (slot + 1) / self.slots) / sum(width)
                    push(dst, ahead + int(per * (u + share)))
                    if done == len(chunks):
                        while due_m:
                            dst.append(("shift", due_m.pop(0)[0], 0))
                if slot == 0:
                    for c in range(2):
                        e = s - self.lag - 2 - self.last_step[c]
                        if e >= 0 and e % ns == 0 and e // ns < self.units:
                            dst.append(("norm", e // ns, c))
        self.ring = self.ring_first + [x for step in self.ring_at for slot in step for x in slot]
        self.ring_len = len(self.ring)
        self.norm_at = [i for i, item in enumerate(self.ring) if item[0] == "norm"]


A0 = Attention("rot", 32, 8, 16, 0.25, 4, True)
A1 = Attention("std", 8, 8, 32, 1.0, 2, False)

FFN_A, QKV0, WO0, FFN_B, MOE_A, QKV1, WO1, MOE_B = range(8)
LN_RANK = {FFN_A: 0, QKV0: 1, FFN_B: 2, MOE_A: 3, QKV1: 4, MOE_B: 5}
UPD_RANK = {FFN_A: 0, WO0: 1, FFN_B: 2, MOE_A: 3, WO1: 4, MOE_B: 5}
BIAS_RANK = {WO0: 0, MOE_A: 1, WO1: 2, MOE_B: 3}
MOE_RANK = {MOE_A: 0, MOE_B: 1}
CHAINS = [[FFN_A, QKV0], [WO0, FFN_B, MOE_A, QKV1], [WO1, MOE_B]]
ATT = {QKV0: A0, QKV1: A1}
WO_ATT = {WO0: A0, WO1: A1}


class Signal:

    def __init__(self, nc, ctx, name, per_seq):
        self.sem = ctx.enter_context(nc.semaphore(name))
        self.per_seq = per_seq

    def at(self, b, n):
        return b * self.per_seq + n


def build(nc, x_in, rope_cos, rope_sin, W, out):
    ctx = ExitStack()
    with ctx:
        def sb(name, shape, dt=F32):
            return ctx.enter_context(nc.sbuf_tensor(name, shape, dt))

        def signal(name, per_seq):
            return Signal(nc, ctx, name, per_seq)

        def wait(eng, sig, b, n):
            if b > 0 or n > 0:
                eng.wait_ge(sig.sem, sig.at(b, n))

        x = sb("x", [P, NT, D])
        features = sb("features", [P, KC * SEQ])
        xT = features[:, :].rearrange("p (k s) -> p k s", k=KC)
        qkT_mem = sb("qkT_mem", [P, 5 * 3 * SEQ], BF16)
        headsT = qkT_mem[:, 0:2 * KC * SEQ].bitcast(F32).rearrange("p (k s) -> p k s", k=KC)
        v_mem = sb("v_mem", [P, NT * 8 * 33])
        probs = sb("probs", [P, 6, 2, HALF])
        aug_mem = sb("aug_mem", [P, 20480], BF16)
        eff = sb("eff", [P, KC, D])
        wqkv = sb("wqkv", [P, KC * 768])
        wo0 = sb("wo0", [P, KC, D])
        wo1 = sb("wo1", [P, 2, D])
        wbase = sb("wbase", [P, KC, D])
        whl = sb("whl", [P, KC, ER + EXPERTS])
        wlora = sb("wlora", [P, D])
        bqkv = {QKV0: sb("bqkv0", [P, A0.feats]), QKV1: sb("bqkv1", [P, A1.feats])}
        bx = {WO0: sb("bo0", [P, D]), WO1: sb("bo1", [P, D]), MOE_A: sb("bbase", [P, D])}
        bx[MOE_B] = bx[MOE_A]
        cos2 = sb("cos2", [P, NT, 16])
        sin2 = sb("sin2", [P, NT, 16])
        identf = sb("identf", [P, P])
        identb = sb("identb", [P, P], BF16)
        causal = sb("causal", [P, P], BF16)
        expert_no = sb("expert_no", [P, EXPERTS])
        minus_half = sb("minus_half", [P, 1])
        ones = sb("ones", [P, P])
        stats = sb("stats", [P, 2, 6])
        mv = sb("mv", [P, 2, 2])
        var_eps = sb("var_eps", [P, 2, 1])
        rstd = sb("rstd", [P, 2, 1])
        top = sb("top", [P, 8])
        top_at = sb("top_at", [P, 8], U32)
        top_atf = sb("top_atf", [P, 2])
        route = sb("route", [P, 8])
        gate = sb("gate", [P, 2, EXPERTS])
        maxes = sb("maxes", [P, 2, 2, 4, NT])
        shifts = sb("shifts", [P, 2, 64], BF16)
        shiftT = sb("shiftT", [64, 2, P], BF16)
        heads_raw = sb("heads_raw", [P, 2, HALF])
        hw_mem = sb("hw_mem", [P, 4, P])
        hw = [hw_mem[:, i, :] for i in range(2)]
        hwT = [hw_mem[:, 2 + i, :] for i in range(2)]
        inv_sum = sb("inv_sum", [P, 16])

        work = aug_mem[:, :].bitcast(F32)
        at = [0]

        def carve(n):
            at[0] += n
            return work[:, at[0] - n:at[0]]
        xn = [carve(D) for _ in range(2)]
        qkv = [carve(768) for _ in range(3)]
        rot = [carve(640) for _ in range(2)]
        rc = carve(640)
        rs = carve(640)
        rest = [carve(640) for _ in range(2)]
        parts = [carve(960).bitcast(BF16).rearrange("p (n f) -> p n f", n=3) for _ in range(3)]
        assert at[0] <= 10240

        def aug_main(a, u):
            if a is A0:
                return aug_mem[:, 5120 * (u % 3):5120 * (u % 3) + 5120].rearrange("p (n s) -> p n s", n=5)
            return aug_mem[:, 4096 * (u % 3):4096 * (u % 3) + 4096].rearrange("p (n s) -> p n s", n=4)

        def aug_rest(u):
            return aug_mem[:, 12288 + 4096 * (u % 2):16384 + 4096 * (u % 2)].rearrange("p (n s) -> p n s", n=4)

        def q_and_k(a, operands):
            return operands[:, 0:a.unit_heads, :], operands[:, a.unit_heads:, :]

        def values(a):
            w = a.dim + 1
            return v_mem[:, 0:NT * 8 * w].rearrange("p (t h w) -> p t h w", t=NT, h=8)

        def qkT(a):
            return qkT_mem[:, 0:a.blocks * 3 * SEQ].rearrange("p (r n s) -> p r n s", r=3, n=a.blocks)

        def qkT_flat(a):
            return qkT_mem[:, 0:a.blocks * 3 * SEQ].rearrange("p (n s) -> p n s", s=SEQ)

        bank = ctx.enter_context(nc.psum_tensor("bank", [P, 8, 512], F32))
        turn = [bank[:, 0, :], bank[:, 1, :]]
        prod = [bank[:, 2:4, :], bank[:, 4:6, :]]
        prod_flat = [p.rearrange("p n c -> p (n c)") for p in prod]
        partT = bank[:, 6:8, :].bitcast(BF16).rearrange("p n (b c) -> p (n b) c", c=P)
        scores = bank[:, 0:4, :]
        ring = [bank[:, 4, :], bank[:, 5, :]]
        heads = [bank[:, 6, :], bank[:, 7, :]]

        s_const = signal("const_ready", 0)
        s_pool = signal("pool_memsets", 0)
        gate_sum = signal("gate_sum", 2 * NT)
        s_w = ctx.enter_context(nc.semaphore("weights_loaded"))
        s_ffn_in = ctx.enter_context(nc.semaphore("ffn_inputs_loaded"))
        s_eff = {n: ctx.enter_context(nc.semaphore(f"eff_{n}")) for n in
                 ("ab", "sum", "sq", "norm", "sqrt", "inv", "scale", "ready", "half_bias")}
        wqkv_loaded = signal("wqkv_loaded", 32)
        x_loaded = [signal(f"x_loaded{t}", 16) for t in range(NT)]
        x_stored = [signal(f"x_stored{t}", 16) for t in range(NT)]
        ln_stat = signal("ln_stat", 6 * NT)
        ln_mv = signal("ln_mv", 6 * NT)
        ln_eps = signal("ln_eps", 6 * NT)
        ln_rstd = signal("ln_rstd", 6 * NT)
        xn_ready = signal("xn_ready", 6 * NT)
        turned = signal("turned", 8 * NT)
        xT_ready = signal("xT_ready", 8 * NT)
        prod_ready = signal("prod_ready", 8 * NT)
        x_new = signal("x_new", 6 * NT)
        x_biased = signal("x_biased", 4 * NT)
        hl_ready = signal("hl_ready", 2 * NT)
        route_step = signal("route_step", 2 * NT * 9)
        route_exp = signal("route_exp", 2 * NT)
        hw_ready = signal("hw_ready", 2 * NT)
        hw_turned = signal("hw_turned", 2 * NT)
        hwT_ready = signal("hwT_ready", 2 * NT)
        qs = {}
        for st, a in ATT.items():
            n = a.name
            s = {}
            s["qkv"] = signal(f"{n}_qkv_ready", NT)
            s["roped"] = signal(f"{n}_roped", NT)
            s["cos"] = signal(f"{n}_cos_product", NT)
            s["sin"] = signal(f"{n}_sin_product", NT)
            s["p1"] = signal(f"{n}_part1", NT)
            s["r1"] = signal(f"{n}_rest1", NT)
            s["p2"] = signal(f"{n}_part2", NT)
            s["p3"] = signal(f"{n}_part3", NT)
            s["v_ones"] = signal(f"{n}_v_ones", 1)
            s["v"] = signal(f"{n}_v_ready", NT)
            s["partT"] = signal(f"{n}_parts_turned", NT)
            s["evA"] = signal(f"{n}_partsT_act", NT)
            s["evB"] = signal(f"{n}_partsT_dve", NT)
            a.main_dmas, a.rest_dmas = len(a.main_loads), len(a.rest_loads)
            s["main"] = [signal(f"{n}_operands{i}", 16 * a.main_dmas * len(range(i, a.units, 3))) for i in range(3)]
            s["rest"] = [signal(f"{n}_rest_operands{i}", 16 * a.rest_dmas * len(range(i, a.units, 2))) for i in range(2)]
            s["ones"] = signal(f"{n}_one_rows", 1)
            s["shift_rows"] = [signal(f"{n}_shift_rows{i}", 32 * len(range(i, a.units, 2))) for i in range(2)]
            s["ring_full"] = signal(f"{n}_ring_full", a.ring_len)
            s["max_done"] = signal(f"{n}_max_done", a.units * len(a.max_chunks))
            s["shift_step"] = signal(f"{n}_shift_step", 2 * a.units)
            s["shift"] = signal(f"{n}_shift_ready", a.units)
            s["shiftT"] = signal(f"{n}_shiftT_ready", a.units)
            ne = a.units * len(a.steps) * a.pairs
            s["scored"] = signal(f"{n}_scores_ready", ne)
            s["exp"] = signal(f"{n}_exp_done", ne)
            s["masked"] = signal(f"{n}_masked", a.units * 8 * a.pairs)
            s["pv"] = signal(f"{n}_values_done", a.units * len(a.steps))
            s["raw"] = signal(f"{n}_heads_raw", a.chunks)
            s["inv"] = signal(f"{n}_inverse_sum", a.chunks)
            s["normed"] = signal(f"{n}_heads_ready", a.chunks)
            qs[st] = s

        def normed(st, b, eng):
            eng.wait_ge(qs[st]["normed"].sem, qs[st]["normed"].at(b, ATT[st].chunks))

        block = ctx.enter_context(nc.Block())
        items = [[(st, t) for st in chain for t in range(NT)] for chain in CHAINS]

        @block.sync
        def _(sp):
            sp.dma_start(eff[:, :, :], W["ffn_w"].rearrange("(k p) n -> p k n", p=P)).then_inc(s_ffn_in, 16)
            sp.dma_start(wlora[0:32, :], W["ffn_a"]).then_inc(s_ffn_in, 16)
            sp.dma_start(wbase[0:32, 0, :], W["ffn_b"]).then_inc(s_ffn_in, 16)
            sp.dma_start(bx[MOE_A][:, :], W["mag"].partition_broadcast(P)).then_inc(s_ffn_in, 16)

            def load_x(b):
                for t in range(NT):
                    wait(sp, x_stored[t], b, 0)
                    sp.dma_start(x[:, t, :], x_in[b, t * P:(t + 1) * P, :]).then_inc(x_loaded[t].sem, 16)

            def store_x(b):
                for t in range(NT):
                    sp.wait_ge(x_new.sem, x_new.at(b, UPD_RANK[MOE_B] * NT + t + 1))
                    sp.dma_start(out[b, t * P:(t + 1) * P, :], x[:, t, :]).then_inc(x_stored[t].sem, 16)

            load_more = [(wo0, W["wo0"], KC), (whl, W["hl"], KC), (wo1, W["wo1"], 2)]

            def load_weights():
                for dst, src, k in load_more:
                    sp.dma_start(dst[:, :, :], src.rearrange("(k p) n -> p k n", p=P)).then_inc(s_w, 16)
                for dst, src in ((bqkv[QKV0], W["bqkv0"]), (bqkv[QKV1], W["bqkv1"]),
                                 (bx[WO0], W["bo0"]), (bx[WO1], W["bo1"])):
                    sp.dma_start(dst[:, :], src.partition_broadcast(P)).then_inc(s_w, 16)
                sp.dma_start(cos2[:, :, :], rope_cos.rearrange("(t p) c -> p t c", p=P)).then_inc(s_w, 16)
                sp.dma_start(sin2[:, :, :], rope_sin.rearrange("(t p) c -> p t c", p=P)).then_inc(s_w, 16)
                sp.wait_ge(s_eff["ready"], 1)
                sp.dma_start(wlora[:, :], W["lora_b"]).then_inc(s_w, 16)
                sp.dma_start(wbase[:, :, :], W["base"].rearrange("(k p) n -> p k n", p=P)).then_inc(s_w, 16)
                sp.dma_start(bx[MOE_A][:, :], W["bbase"].partition_broadcast(P)).then_inc(s_w, 16)

            def load_wqkv(b, st):
                n = 0 if st == QKV0 else 1
                wait(sp, prod_ready, b, (QKV0 + 1) * NT if st == QKV1 else (QKV1 + 1 - 8) * NT)
                a = ATT[st]
                sp.dma_start(wqkv[:, 0:KC * a.feats].rearrange("p (k n) -> p k n", k=KC),
                             W[f"wqkv{n}"].rearrange("(k p) n -> p k n", p=P)).then_inc(wqkv_loaded.sem, 16)

            def load_parts(a, dst, loads, u, sem):
                src = qkT(a)
                f = u * a.dim
                for i, part, first, n in loads:
                    sp.dma_start(dst[a.dim * i:a.dim * (i + 1), first:first + n, :],
                                 src[f:f + a.dim, part - 1, first:first + n, :]).then_inc(sem, 16)

            def load_operands(b, st, u):
                a, s = ATT[st], qs[st]
                if u >= 3:
                    sp.wait_ge(s["pv"].sem, s["pv"].at(b, (u - 2) * len(a.steps)))
                load_parts(a, aug_main(a, u), a.main_loads, u, s["main"][u % 3].sem)

            def load_rest(b, st, u):
                a, s = ATT[st], qs[st]
                if u >= 2:
                    sp.wait_ge(s["pv"].sem, s["pv"].at(b, (u - 1) * len(a.steps)))
                load_parts(a, aug_rest(u), a.rest_loads, u, s["rest"][u % 2].sem)

            def load_shift(b, st, u):
                a, s = ATT[st], qs[st]
                q, _ = q_and_k(a, aug_main(a, u))
                n = a.unit_heads * NT
                sp.wait_ge(s["shiftT"].sem, s["shiftT"].at(b, u + 1))
                for part in range(2):
                    sp.dma_start(q[96 + part:97 + part, :, :].rearrange("o h (t s) -> o (h t) s", s=P),
                                 shiftT[part * n:(part + 1) * n, u % 2, :]
                                 ).then_inc(s["shift_rows"][u % 2].sem, 16)

            def attention(b, st):
                a, s = ATT[st], qs[st]
                sp.wait_ge(s["evA"].sem, s["evA"].at(b, NT))
                sp.wait_ge(s["evB"].sem, s["evB"].at(b, NT))
                for u in range(3):
                    load_operands(b, st, u)
                    if a.rest_parts and u < 2:
                        load_rest(b, st, u)
                load_shift(b, st, 0)
                for u in range(a.units):
                    if u + 1 < a.units:
                        load_shift(b, st, u + 1)
                    if u + 3 < a.units:
                        load_operands(b, st, u + 3)
                    if a.rest_parts and u + 2 < a.units:
                        load_rest(b, st, u + 2)

            for b in range(BATCH):
                load_x(b)
                load_wqkv(b, QKV0)
                if b == 0:
                    load_weights()
                attention(b, QKV0)
                load_wqkv(b, QKV1)
                attention(b, QKV1)
                store_x(b)
            for t in range(NT):
                sp.wait_ge(x_stored[t].sem, x_stored[t].at(BATCH, 0))

        @block.tensor
        def _(pe):
            mm = nc.tensor.matmul
            pe.wait_ge(s_ffn_in, 64)
            pe.wait_ge(s_const.sem, 8)
            for k in range(KC):
                mm(bank[:, k, :], wlora[0:32, k * P:(k + 1) * P], wbase[0:32, 0, :], start=True, stop=True
                   ).then_inc(s_eff["ab"], 1)
            for k in range(KC):
                pe.wait_ge(s_eff["sq"], k + 1)
                last = mm(bank[:, 4, :], ones[:], probs[:, k, 0, :], start=(k == 0), stop=(k == KC - 1))
            last.then_inc(s_eff["norm"], 1)

            def turn_x(b, st, t):
                n = st * NT + t
                if st in WO_ATT:
                    if t == 0:
                        normed(QKV0 if st == WO0 else QKV1, b, pe)
                    src = features[:, t * D:(t + 1) * D]
                    kc = KC if st == WO0 else 2
                else:
                    pe.wait_ge(xn_ready.sem, xn_ready.at(b, LN_RANK[st] * NT + t + 1))
                    src, kc = xn[n % 2], KC
                wait(pe, xT_ready, b, n - 1)
                for k in range(kc):
                    last = nc.tensor.transpose(turn[n % 2][:, k * P:(k + 1) * P], src[:, k * P:(k + 1) * P], identf[:])
                last.then_inc(turned.sem, 1)

            def begin(b, st, t):
                n = st * NT + t
                pe.wait_ge(xT_ready.sem, xT_ready.at(b, n + 1))
                if n >= 2:
                    st2, t2 = divmod(n - 2, NT)
                    read, m = (qs[st2]["qkv"], t2 + 1) if st2 in ATT else (x_new, UPD_RANK[st2] * NT + t2 + 1)
                    wait(pe, read, b, m)
                else:
                    wait(pe, x_new, b, n - 1)
                return n

            def product(b, st, t):
                n = st * NT + t
                if st in MOE_RANK:
                    for k in range(KC):
                        last = mm(prod[n % 2][:, 0, :], xT[:, k, t * P:(t + 1) * P], wbase[:, k, :],
                                  start=(k == 0), stop=False)
                    return
                begin(b, st, t)
                if st in ATT:
                    a = ATT[st]
                    if t == 0:
                        q = 1 if st == QKV0 else 2
                        pe.wait_ge(wqkv_loaded.sem, wqkv_loaded.at(b, 16 * q))
                    w = wqkv[:, 0:KC * a.feats].rearrange("p (k n) -> p k n", k=KC)
                    for c in range(2):
                        lo, hi = c * 512, min(a.feats, (c + 1) * 512)
                        for k in range(KC):
                            last = mm(prod[n % 2][:, c, 0:hi - lo], xT[:, k, t * P:(t + 1) * P], w[:, k, lo:hi],
                                      start=(k == 0), stop=(k == KC - 1))
                    last.then_inc(prod_ready.sem, 1)
                else:
                    w = {FFN_A: eff, FFN_B: eff, WO0: wo0, WO1: wo1}[st]
                    src = headsT if st in WO_ATT else xT
                    kc = 2 if st == WO1 else KC
                    for k in range(kc):
                        last = mm(prod[n % 2][:, 0, :], src[:, k, t * P:(t + 1) * P], w[:, k, :],
                                  start=(k == 0), stop=(k == kc - 1))
                    last.then_inc(prod_ready.sem, 1)

            def router(b, st, t):
                n = begin(b, st, t)
                for k in range(KC):
                    last = mm(prod[n % 2][:, 1, 0:ER + EXPERTS], xT[:, k, t * P:(t + 1) * P], whl[:, k, :],
                              start=(k == 0), stop=(k == KC - 1))
                last.then_inc(hl_ready.sem, 1)

            def turn_hw(b, st, t):
                n, r = st * NT + t, MOE_RANK[st] * NT + t
                pe.wait_ge(hw_ready.sem, hw_ready.at(b, r + 1))
                nc.tensor.transpose(prod[n % 2][:, 1, 256:256 + P], hw[r % 2], identf[:]).then_inc(hw_turned.sem, 1)

            def lora(b, st, t):
                n, r = st * NT + t, MOE_RANK[st] * NT + t
                pe.wait_ge(hwT_ready.sem, hwT_ready.at(b, r + 1))
                mm(prod[n % 2][:, 0, :], hwT[r % 2], wlora[:, :], start=False, stop=True).then_inc(prod_ready.sem, 1)

            def turn_parts(b, st, t):
                a, s = ATT[st], qs[st]
                pe.wait_ge(s["p3"].sem, s["p3"].at(b, t + 1))
                if t > 0:
                    pe.wait_ge(s["evA"].sem, s["evA"].at(b, t))
                    pe.wait_ge(s["evB"].sem, s["evB"].at(b, t))
                for m in range(3):
                    for f in range(a.blocks):
                        last = nc.tensor.transpose(partT[:, m * a.blocks + f, :], parts[t % 3][:, m, f * P:(f + 1) * P],
                                                   identb[:])
                last.then_inc(s["partT"].sem, 1)

            def chain(b, its):
                for i in range(len(its) + 6):
                    if i < len(its):
                        turn_x(b, *its[i])
                    if 2 <= i < len(its) + 2 and its[i - 2][0] in MOE_RANK:
                        turn_hw(b, *its[i - 2])
                    if 1 <= i < len(its) + 1 and its[i - 1][0] in MOE_RANK:
                        router(b, *its[i - 1])
                    if 2 <= i < len(its) + 2 and its[i - 2][0] in MOE_RANK:
                        lora(b, *its[i - 2])
                    if 1 <= i < len(its) + 1:
                        product(b, *its[i - 1])
                    if 5 <= i < len(its) + 5 and its[i - 5][0] in ATT:
                        turn_parts(b, *its[i - 5])

            def attention(b, st):
                a, s = ATT[st], qs[st]
                ns = len(a.steps)
                v = values(a)
                count = {"ring": 0, "diag": 0}

                def ring_item(kind, u, n):
                    i = count["ring"]
                    count["ring"] += 1
                    dst = ring[i % 2]
                    q, k = q_and_k(a, aug_main(a, u))
                    if i >= 2:
                        s_free(i)
                    if kind == "max":
                        t, kp, w, h0, nh = a.max_chunks[n]
                        if n == 0:
                            m = s["main"][u % 3]
                            pe.wait_ge(m.sem, m.at(b, 16 * a.main_dmas * (u // 3 + 1)))
                        diag = kp == 1 or t < 4
                        for h in range(nh):
                            last = mm(dst[:, h * w:(h + 1) * w], q[0:96, h0 + h, t * P:(t + 1) * P],
                                      k[0:96, (h0 + h) % a.k_copies, kp * HALF:kp * HALF + w],
                                      start=True, stop=not diag)
                            if diag:
                                last = mm(dst[:, (h + 1) * w - P:(h + 1) * w], identb[:], causal[:],
                                          start=False, stop=True)
                    elif kind == "shift":
                        m = 2 * a.unit_heads * NT
                        pe.wait_ge(s["shift"].sem, s["shift"].at(b, u + 1))
                        last = nc.tensor.transpose(dst[0:m, 0:P // 2].bitcast(BF16), shifts[:, u % 2, 0:m], identb[:])
                    else:
                        c = 2 * u + n
                        pe.wait_ge(s["raw"].sem, s["raw"].at(b, c + 1))
                        for j in range(4):
                            last = nc.tensor.transpose(dst[:, j * P:(j + 1) * P],
                                                       heads_raw[:, c % 2, j * P:(j + 1) * P], identf[:])
                    last.then_inc(s["ring_full"].sem, 1)

                def s_free(i):
                    kind, u, n = a.ring[i - 2]
                    read, m = {"max": (s["max_done"], u * len(a.max_chunks) + n + 1), "shift": (s["shiftT"], u + 1),
                               "norm": (s["normed"], 2 * u + n + 1)}[kind]
                    pe.wait_ge(read.sem, read.at(b, m))

                def score(g, first, last_):
                    u, k_ = divmod(g, ns)
                    c, j, q0, w = a.steps[k_]
                    q, k = q_and_k(a, aug_main(a, u))
                    if k_ == 0 and first == 0:
                        sr = s["shift_rows"][u % 2]
                        pe.wait_ge(sr.sem, sr.at(b, 32 * (u // 2 + 1)))
                        if a.rest_parts:
                            m = s["rest"][u % 2]
                            pe.wait_ge(m.sem, m.at(b, 16 * a.rest_dmas * (u // 2 + 1)))
                    for h in range(first, last_):
                        e = g * a.pairs + h // 2
                        if e >= 2 and h % 2 == 0:
                            pe.wait_ge(s["exp"].sem, s["exp"].at(b, e - 1))
                        dst = scores[:, 2 * (e % 2) + h % 2, 0:w]
                        last = mm(dst, k[0:98, h % a.k_copies, j * P:(j + 1) * P], q[0:98, h, q0:q0 + w],
                                  start=True, stop=not a.rest_parts)
                        if a.rest_parts:
                            q2, k2 = q_and_k(a, aug_rest(u))
                            last = mm(dst, k2[0:96, h, j * P:(j + 1) * P], q2[0:96, h, q0:q0 + w],
                                      start=False, stop=True)
                        if h % 2 == 1:
                            last.then_inc(s["scored"].sem, 1)

                def value(g):
                    u, k_ = divmod(g, ns)
                    c, j, q0, w = a.steps[k_]
                    ch = 2 * u + c
                    e = g * a.pairs
                    if j >= 4 * c:
                        count["diag"] += a.pairs
                        pe.wait_ge(s["masked"].sem, s["masked"].at(b, count["diag"]))
                    pe.wait_ge(s["exp"].sem, s["exp"].at(b, e + a.pairs))
                    if j == 0 and ch >= 2:
                        pe.wait_ge(s["raw"].sem, s["raw"].at(b, ch - 1))
                    for h in range(a.unit_heads):
                        kv = u if a.grouped else u * a.unit_heads + h
                        last = mm(heads[ch % 2][a.rows * h:a.rows * h + a.dim + 1, q0 - HALF * c:HALF],
                                  v[:, j, kv, :], probs[:, (e + h // 2) % 6, h % 2, 0:w],
                                  start=(j == 0), stop=(j == 4 * c + 3))
                    last.then_inc(s["pv"].sem, 1)

                pe.wait_ge(s["ones"].sem, s["ones"].at(b, 1))
                pe.wait_ge(s["v_ones"].sem, s["v_ones"].at(b, 1))
                pe.wait_ge(s["v"].sem, s["v"].at(b, NT))
                for it in a.ring_first:
                    ring_item(*it)
                for g in range(a.units * ns + a.lag + 4):
                    half = a.unit_heads // 2
                    if g < a.units * ns:
                        score(g, 0, half)
                    for it in a.ring_at[g][0]:
                        ring_item(*it)
                    if g < a.units * ns:
                        score(g, half, a.unit_heads)
                    for it in a.ring_at[g][1]:
                        ring_item(*it)
                    if a.lag <= g < a.units * ns + a.lag:
                        value(g - a.lag)
                    for it in a.ring_at[g][2]:
                        ring_item(*it)

            pe.wait_ge(s_eff["ready"], 1)
            pe.wait_ge(s_w, 16 * 12)
            for b in range(BATCH):
                chain(b, items[0])
                attention(b, QKV0)
                chain(b, items[1])
                attention(b, QKV1)
                chain(b, items[2])

        @block.vector
        def _(dve):
            V = nc.vector
            V.memset(minus_half[:], -0.5).then_inc(s_const.sem, 1)
            V.memset(ones[:], 1.0).then_inc(s_const.sem, 1)
            V.memset(heads[0], 0.0).then_inc(s_const.sem, 1)
            V.memset(heads[1], 0.0).then_inc(s_const.sem, 1)
            dve.wait_ge(s_ffn_in, 64)
            for k in range(KC):
                dve.wait_ge(s_eff["ab"], k + 1)
                V.tensor_tensor(eff[:, k, :], bank[:, k, :], eff[:, k, :], ALU.add).then_inc(s_eff["sum"], 1)
            for k in range(KC):
                dve.wait_ge(s_eff["sum"], k + 1)
                V.tensor_tensor(probs[:, k, 0, :], eff[:, k, :], eff[:, k, :], ALU.mult).then_inc(s_eff["sq"], 1)
            dve.wait_ge(s_eff["sqrt"], 1)
            V.reciprocal(probs[:, 5, 0, :], probs[:, 4, 0, :]).then_inc(s_eff["inv"], 1)
            dve.wait_ge(s_eff["inv"], 1)
            V.scalar_tensor_tensor(probs[:, 5, 1, :], probs[:, 5, 0, :], 0.5, bx[MOE_A][:, :], ALU.mult, ALU.mult
                                   ).then_inc(s_eff["scale"], 1)
            dve.wait_ge(s_eff["scale"], 1)
            for k in range(KC):
                last = V.tensor_tensor(eff[:, k, :], eff[:, k, :], probs[:, 5, 1, :], ALU.mult)
            last.then_inc(s_eff["ready"], 1)
            dve.wait_ge(s_w, 16 * 12)
            V.tensor_scalar(bx[MOE_A][:, :], bx[MOE_A][:, :], 0.5, None, ALU.mult).then_inc(s_eff["half_bias"], 1)

            def layernorm(b, st, t):
                if st not in LN_RANK:
                    return
                l = LN_RANK[st]
                n = l * NT + t
                i = (st * NT + t) % 2
                if l == 0:
                    dve.wait_ge(x_loaded[t].sem, x_loaded[t].at(b, 16))
                else:
                    dve.wait_ge(x_new.sem, x_new.at(b, (l - 1) * NT + t + 1))
                V.bn_stats(stats[:, i, :], x[:, t, :]).then_inc(ln_stat.sem, 1)
                dve.wait_ge(ln_stat.sem, ln_stat.at(b, n + 1))
                V.bn_aggr(mv[:, i, :], stats[:, i, :]).then_inc(ln_mv.sem, 1)
                dve.wait_ge(ln_mv.sem, ln_mv.at(b, n + 1))
                V.tensor_scalar(var_eps[:, i, :], mv[:, i, 1:2], EPS, None, ALU.add).then_inc(ln_eps.sem, 1)
                dve.wait_ge(ln_rstd.sem, ln_rstd.at(b, n + 1))
                wait(dve, turned, b, st * NT + t - 1)
                V.tensor_scalar(xn[i], x[:, t, :], mv[:, i, 0:1], rstd[:, i, :], ALU.subtract, ALU.mult
                                ).then_inc(xn_ready.sem, 1)

            def epilogue(b, st, t):
                n = st * NT + t
                dve.wait_ge(prod_ready.sem, prod_ready.at(b, n + 1))
                if st in ATT:
                    a, s = ATT[st], qs[st]
                    if t >= 3:
                        dve.wait_ge(s["v"].sem, s["v"].at(b, t - 2))
                        dve.wait_ge(s["roped"].sem if a.rope else s["p1"].sem, s["p1"].at(b, t - 2))
                        if not a.rope:
                            dve.wait_ge(s["r1"].sem, s["r1"].at(b, t - 2))
                    V.tensor_tensor(qkv[t % 3][:, 0:a.feats], prod_flat[n % 2][:, 0:a.feats], bqkv[st][:, :], ALU.add
                                    ).then_inc(s["qkv"].sem, 1)
                    return
                if st in BIAS_RANK:
                    dve.wait_ge(x_biased.sem, x_biased.at(b, BIAS_RANK[st] * NT + t + 1))
                    scale = 0.5 if st in MOE_RANK else 1.0
                    V.scalar_tensor_tensor(x[:, t, :], prod[n % 2][:, 0, :], scale, x[:, t, :], ALU.mult, ALU.add
                                           ).then_inc(x_new.sem, 1)
                else:
                    V.tensor_tensor(x[:, t, :], prod[n % 2][:, 0, :], x[:, t, :], ALU.add
                                    ).then_inc(x_new.sem, 1)

            def routing(b, st, t):
                n, r = st * NT + t, MOE_RANK[st] * NT + t
                logits = prod[n % 2][:, 1, ER:ER + EXPERTS]
                step = [9 * r]

                def link(ins):
                    step[0] += 1
                    ins.then_inc(route_step.sem, 1)
                    dve.wait_ge(route_step.sem, route_step.at(b, step[0]))
                dve.wait_ge(hl_ready.sem, hl_ready.at(b, r + 1))
                link(V.max(top[:], logits))
                link(V.tensor_tensor(route[:, 0:1], top[:, 1:2], top[:, 0:1], ALU.subtract))
                link(V.max_index(top_at[:], top[:], logits))
                link(V.tensor_copy(top_atf[:], top_at[:, 0:2]))
                dve.wait_ge(route_exp.sem, route_exp.at(b, r + 1))
                link(V.tensor_scalar(route[:, 2:3], route[:, 1:2], 1.0, 0.5, ALU.add, ALU.mult))
                link(V.reciprocal(route[:, 3:4], route[:, 2:3]))
                link(V.tensor_tensor(route[:, 4:5], route[:, 1:2], route[:, 3:4], ALU.mult))
                link(V.tensor_scalar(gate[:, 0, :], expert_no[:], top_atf[:, 0:1], route[:, 3:4], ALU.is_equal, ALU.mult))
                link(V.tensor_scalar(gate[:, 1, :], expert_no[:], top_atf[:, 1:2], route[:, 4:5], ALU.is_equal, ALU.mult))

            def weigh(b, st, t):
                n, r = st * NT + t, MOE_RANK[st] * NT + t
                V.tensor_tensor(gate[:, 0, :], gate[:, 0, :], gate[:, 1, :], ALU.add).then_inc(gate_sum.sem, 1)
                dve.wait_ge(gate_sum.sem, gate_sum.at(b, r + 1))
                wait(dve, hw_turned, b, r - 1)
                V.tensor_tensor(hw[r % 2].rearrange("p (e r) -> p e r", e=EXPERTS),
                                prod[n % 2][:, 1, 0:ER].rearrange("p (e r) -> p e r", e=EXPERTS),
                                gate[:, 0, :].unsqueeze(2).to_broadcast([P, EXPERTS, RANK]), ALU.mult
                                ).then_inc(hw_ready.sem, 1)

            def rope_cos_part(b, st, t):
                a, s = ATT[st], qs[st]
                if a.rope:
                    dve.wait_ge(s["qkv"].sem, s["qkv"].at(b, t + 1))
                    V.tensor_tensor(rc.rearrange("p (h d) -> p h d", d=16),
                                    qkv[t % 3][:, 0:a.qk_feats].rearrange("p (h d) -> p h d", d=16),
                                    cos2[:, t, :].unsqueeze(1).to_broadcast([P, a.qk_feats // 16, 16]), ALU.mult
                                    ).then_inc(s["cos"].sem, 1)

            def rope_sum(b, st, t):
                a, s = ATT[st], qs[st]
                if a.rope:
                    dve.wait_ge(s["cos"].sem, s["cos"].at(b, t + 1))
                    dve.wait_ge(s["sin"].sem, s["sin"].at(b, t + 1))
                    V.tensor_tensor(rot[t % 2], rc, rs, ALU.add).then_inc(s["roped"].sem, 1)

            def rest1(b, st, t):
                a, s = ATT[st], qs[st]
                src = rot[t % 2] if a.rope else qkv[t % 3]
                dve.wait_ge(s["p1"].sem, s["p1"].at(b, t + 1))
                if t >= 2:
                    dve.wait_ge(s["p3"].sem, s["p3"].at(b, t - 1))
                V.tensor_tensor(rest[t % 2][:, 0:a.qk_feats], src[:, 0:a.qk_feats], parts[t % 3][:, 0, 0:a.qk_feats],
                                ALU.subtract).then_inc(s["r1"].sem, 1)

            def evacuate(b, st, t):
                a, s = ATT[st], qs[st]
                dve.wait_ge(s["partT"].sem, s["partT"].at(b, t + 1))
                n = 3 * a.blocks - 8
                V.tensor_copy(qkT_flat(a)[:, 8:8 + n, t * P:(t + 1) * P], partT[:, 8:8 + n, :]
                              ).then_inc(s["evB"].sem, 1)

            def chain(b, its):
                layernorm(b, *its[0])
                for i in range(len(its) + 7):
                    if i + 1 < len(its):
                        layernorm(b, *its[i + 1])
                    if 3 <= i < len(its) + 3 and its[i - 3][0] in ATT:
                        rope_sum(b, *its[i - 3])
                    if 2 <= i < len(its) + 2:
                        epilogue(b, *its[i - 2])
                        if its[i - 2][0] in ATT:
                            rope_cos_part(b, *its[i - 2])
                    if 1 <= i < len(its) + 1 and its[i - 1][0] in MOE_RANK:
                        routing(b, *its[i - 1])
                        weigh(b, *its[i - 1])
                    if 3 <= i < len(its) + 3 and its[i - 3][0] in ATT:
                        rest1(b, *its[i - 3])
                    if 6 <= i < len(its) + 6 and its[i - 6][0] in ATT:
                        evacuate(b, *its[i - 6])

            def attention(b, st):
                a, s = ATT[st], qs[st]
                for i, (kind, u, n) in enumerate(a.ring):
                    src = ring[i % 2]
                    dve.wait_ge(s["ring_full"].sem, s["ring_full"].at(b, i + 1))
                    if kind == "max":
                        t, kp, w, h0, nh = a.max_chunks[n]
                        V.tensor_reduce(maxes[:, u % 2, kp, h0:h0 + nh, t],
                                        src[:, 0:nh * w].rearrange("p (h w) -> p h w", h=nh), AX.X, ALU.max
                                        ).then_inc(s["max_done"].sem, 1)
                        if n == len(a.max_chunks) - 1:
                            shift_parts(b, st, u)
                    elif kind == "shift":
                        m = 2 * a.unit_heads * NT
                        if u >= 2:
                            sr = s["shift_rows"][u % 2]
                            dve.wait_ge(sr.sem, sr.at(b, 32 * (u // 2)))
                        V.tensor_copy(shiftT[0:m, u % 2, :], src[0:m, 0:P // 2].bitcast(BF16)
                                      ).then_inc(s["shiftT"].sem, 1)
                    else:
                        c = 2 * u + n
                        nh, d = a.unit_heads, a.dim
                        blocks = src.rearrange("p (g r) -> p g r", r=a.rows)
                        wait(dve, s["normed"], b, c)
                        V.reciprocal(inv_sum[:, 0:4 * nh].unsqueeze(2), blocks[:, :, d:d + 1]).then_inc(s["inv"].sem, 1)
                        dve.wait_ge(s["inv"].sem, s["inv"].at(b, c + 1))
                        width = a.q_feats
                        dst = features[:, :].rearrange("p (t f) -> p t f", f=D)[
                            :, 4 * n:4 * n + 4, u * nh * d:(u + 1) * nh * d].rearrange("p t (h d) -> p t h d", h=nh)
                        V.tensor_tensor(dst, src.rearrange("p (t h r) -> p t h r", t=4, h=nh)[:, :, :, 0:d],
                                        inv_sum[:, 0:4 * nh].rearrange("p (t h) -> p t h", t=4).unsqueeze(3)
                                        .to_broadcast([P, 4, nh, d]), ALU.mult).then_inc(s["normed"].sem, 1)

            def shift_parts(b, st, u):
                a, s = ATT[st], qs[st]
                nh, m = a.unit_heads, a.unit_heads * NT
                mx = maxes[:, u % 2, 0, 0:nh, :]
                dve.wait_ge(s["max_done"].sem, s["max_done"].at(b, (u + 1) * len(a.max_chunks)))
                V.tensor_tensor(maxes[:, u % 2, 0, 0:nh, 4:8], maxes[:, u % 2, 0, 0:nh, 4:8],
                                maxes[:, u % 2, 1, 0:nh, 4:8], ALU.max).then_inc(s["shift_step"].sem, 1)
                dve.wait_ge(s["shift_step"].sem, s["shift_step"].at(b, 2 * u + 1))
                hi = shifts[:, u % 2, 0:m].rearrange("p (h t) -> p h t", h=nh)
                lo = shifts[:, u % 2, m:2 * m].rearrange("p (h t) -> p h t", h=nh)
                V.tensor_scalar(hi, mx, -1.0, None, ALU.mult).then_inc(s["shift_step"].sem, 1)
                dve.wait_ge(s["shift_step"].sem, s["shift_step"].at(b, 2 * u + 2))
                V.scalar_tensor_tensor(lo, mx, -1.0, hi, ALU.mult, ALU.subtract).then_inc(s["shift"].sem, 1)

            for b in range(BATCH):
                chain(b, items[0])
                attention(b, QKV0)
                chain(b, items[1])
                attention(b, QKV1)
                chain(b, items[2])

        @block.scalar
        def _(act):
            A = nc.scalar
            act.wait_ge(s_eff["norm"], 1)
            A.activation(probs[:, 4, 0, :], bank[:, 4, :], ACT.Sqrt).then_inc(s_eff["sqrt"], 1)

            def copy_turned(b, st, t):
                n = st * NT + t
                kc = 2 if st == WO1 else KC
                act.wait_ge(turned.sem, turned.at(b, n + 1))
                dst = headsT if st in WO_ATT else xT
                A.copy(dst[:, 0:kc, t * P:(t + 1) * P],
                       turn[n % 2][:, 0:kc * P].rearrange("p (k c) -> p k c", k=kc)).then_inc(xT_ready.sem, 1)

            def gate_exp(b, st, t):
                r = MOE_RANK[st] * NT + t
                act.wait_ge(route_step.sem, route_step.at(b, 9 * r + 2))
                A.activation(route[:, 1:2], route[:, 0:1], ACT.Exp).then_inc(route_exp.sem, 1)

            def copy_hw(b, st, t):
                n, r = st * NT + t, MOE_RANK[st] * NT + t
                act.wait_ge(hw_turned.sem, hw_turned.at(b, r + 1))
                A.copy(hwT[r % 2], prod[n % 2][:, 1, 256:256 + P]).then_inc(hwT_ready.sem, 1)

            def part1(b, st, t):
                a, s = ATT[st], qs[st]
                act.wait_ge(s["roped"].sem if a.rope else s["qkv"].sem, s["qkv"].at(b, t + 1))
                if t >= 3:
                    act.wait_ge(s["partT"].sem, s["partT"].at(b, t - 2))
                src = rot[t % 2] if a.rope else qkv[t % 3]
                A.copy(parts[t % 3][:, 0, 0:a.qk_feats], src[:, 0:a.qk_feats]).then_inc(s["p1"].sem, 1)

            def part2(b, st, t):
                a, s = ATT[st], qs[st]
                act.wait_ge(s["r1"].sem, s["r1"].at(b, t + 1))
                A.copy(parts[t % 3][:, 1, 0:a.qk_feats], rest[t % 2][:, 0:a.qk_feats]).then_inc(s["p2"].sem, 1)

            def evacuate(b, st, t):
                a, s = ATT[st], qs[st]
                act.wait_ge(s["partT"].sem, s["partT"].at(b, t + 1))
                A.copy(qkT_flat(a)[:, 0:8, t * P:(t + 1) * P], partT[:, 0:8, :]).then_inc(s["evA"].sem, 1)

            def chain(b, its):
                for i in range(len(its) + 7):
                    if i < len(its):
                        copy_turned(b, *its[i])
                    if 2 <= i < len(its) + 2 and its[i - 2][0] in MOE_RANK:
                        copy_hw(b, *its[i - 2])
                    if 6 <= i < len(its) + 6 and its[i - 6][0] in ATT:
                        evacuate(b, *its[i - 6])
                    if 1 <= i < len(its) + 1 and its[i - 1][0] in MOE_RANK:
                        gate_exp(b, *its[i - 1])
                    if 3 <= i < len(its) + 3 and its[i - 3][0] in ATT:
                        part1(b, *its[i - 3])
                    if 4 <= i < len(its) + 4 and its[i - 4][0] in ATT:
                        part2(b, *its[i - 4])

            def attention(b, st):
                a, s = ATT[st], qs[st]
                ns = len(a.steps)
                for g in range(a.units * ns + a.lag + 2):
                    if g < a.units * ns:
                        c, j, q0, w = a.steps[g % ns]
                        for pr in range(a.pairs):
                            e = g * a.pairs + pr
                            act.wait_ge(s["scored"].sem, s["scored"].at(b, e + 1))
                            if e >= 6:
                                act.wait_ge(s["pv"].sem, s["pv"].at(b, (e - 6) // a.pairs + 1))
                            A.activation(probs[:, e % 6, :, 0:w], scores[:, 2 * (e % 2):2 * (e % 2) + 2, 0:w], ACT.Exp,
                                         scale=a.scale).then_inc(s["exp"].sem, 1)
                    for c in range(2):
                        e = g - a.lag - 1 - a.last_step[c]
                        if e >= 0 and e % ns == 0 and e // ns < a.units:
                            ch = 2 * (e // ns) + c
                            act.wait_ge(s["pv"].sem, s["pv"].at(b, e + a.last_step[c] + 1))
                            if ch >= 2:
                                act.wait_ge(s["ring_full"].sem, s["ring_full"].at(b, a.norm_at[ch - 2] + 1))
                            A.copy(heads_raw[:, ch % 2, :], heads[ch % 2]).then_inc(s["raw"].sem, 1)

            for b in range(BATCH):
                chain(b, items[0])
                attention(b, QKV0)
                chain(b, items[1])
                attention(b, QKV1)
                chain(b, items[2])

        @block.gpsimd
        def _(pool):
            G = nc.gpsimd

            def mask_tile(tile, fill_first, op, fill, i):
                G.memset(tile[:, :], fill_first).then_inc(s_pool.sem, 1)
                pool.wait_ge(s_pool.sem, i)
                return G.affine_select(out=tile[:, :], in_=tile[:, :], compare_op=op, fill=fill, base=0,
                                       pattern=[[-1, P]], channel_multiplier=1)
            mask_tile(identf, 0.0, ALU.not_equal, 1.0, 1).then_inc(s_const.sem, 1)
            mask_tile(identb, 0.0, ALU.not_equal, 1.0, 2).then_inc(s_const.sem, 1)
            mask_tile(causal, 0.0, ALU.is_ge, NEG, 3).then_inc(s_const.sem, 1)
            G.iota(expert_no[:], pattern=[[1, EXPERTS]], base=0, channel_multiplier=0,
                   allow_small_or_imprecise_dtypes=True).then_inc(s_const.sem, 1)
            pool.wait_ge(s_const.sem, 8)

            pool.wait_ge(s_w, 16 * 12)
            pool.wait_ge(s_eff["half_bias"], 1)

            def rstd_of(b, st, t):
                if st not in LN_RANK:
                    return
                n = LN_RANK[st] * NT + t
                i = (st * NT + t) % 2
                pool.wait_ge(ln_eps.sem, ln_eps.at(b, n + 1))
                G.tensor_tensor(rstd[:, i, :], var_eps[:, i, :], minus_half[:, :], ALU.pow).then_inc(ln_rstd.sem, 1)

            def bias_x(b, st, t):
                if st not in BIAS_RANK:
                    return
                if st in LN_RANK:
                    pool.wait_ge(xn_ready.sem, xn_ready.at(b, LN_RANK[st] * NT + t + 1))
                else:
                    pool.wait_ge(x_new.sem, x_new.at(b, (UPD_RANK[st] - 1) * NT + t + 1))
                G.tensor_tensor(x[:, t, :], x[:, t, :], bx[st][:, :], ALU.add).then_inc(x_biased.sem, 1)

            def rope(b, st, t):
                a, s = ATT[st], qs[st]
                if not a.rope:
                    return
                n = a.qk_feats // 16
                pool.wait_ge(s["qkv"].sem, s["qkv"].at(b, t + 1))
                src = qkv[t % 3][:, 0:a.qk_feats]
                if t >= 1:
                    pool.wait_ge(s["roped"].sem, s["roped"].at(b, t))
                for im in range(2):
                    o = rs.rearrange("p (h d c) -> p h d c", d=8, c=2)[:, :, :, im]
                    i_ = src.rearrange("p (h d c) -> p h d c", d=8, c=2)[:, :, :, 1 - im]
                    sn = sin2[:, t, :].rearrange("p (d c) -> p d c", c=2)[:, :, im].unsqueeze(1).to_broadcast([P, n, 8])
                    last = G.tensor_tensor(o, i_, sn, ALU.mult)
                last.then_inc(s["sin"].sem, 1)

            def copy_v(b, st, t):
                a, s = ATT[st], qs[st]
                pool.wait_ge(s["qkv"].sem, s["qkv"].at(b, t + 1))
                v = values(a)
                if t == 0:
                    G.memset(v[:, :, :, a.dim:a.dim + 1], 1.0).then_inc(s["v_ones"].sem, 1)
                G.tensor_copy(v[:, t, :, 0:a.dim],
                              qkv[t % 3][:, a.qk_feats:a.feats].rearrange("p (h d) -> p h d", h=8)
                              ).then_inc(s["v"].sem, 1)

            def part3(b, st, t):
                a, s = ATT[st], qs[st]
                pool.wait_ge(s["p2"].sem, s["p2"].at(b, t + 1))
                G.tensor_tensor(parts[t % 3][:, 2, 0:a.qk_feats], rest[t % 2][:, 0:a.qk_feats],
                                parts[t % 3][:, 1, 0:a.qk_feats], ALU.subtract).then_inc(s["p3"].sem, 1)

            def chain(b, its):
                rstd_of(b, *its[0])
                for i in range(len(its) + 7):
                    if i + 1 < len(its):
                        rstd_of(b, *its[i + 1])
                    if i < len(its):
                        bias_x(b, *its[i])
                    if 2 <= i < len(its) + 2 and its[i - 2][0] in ATT:
                        rope(b, *its[i - 2])
                        copy_v(b, *its[i - 2])
                    if 4 <= i < len(its) + 4 and its[i - 4][0] in ATT:
                        part3(b, *its[i - 4])

            def attention(b, st):
                a, s = ATT[st], qs[st]
                pool.wait_ge(s["partT"].sem, s["partT"].at(b, NT))
                for u in range(3):
                    _, k = q_and_k(a, aug_main(a, u))
                    last = G.memset(k[96:98, :, :], 1.0)
                last.then_inc(s["ones"].sem, 1)
                for g in range(a.units * len(a.steps)):
                    c, j, q0, w = a.steps[g % len(a.steps)]
                    if j < 4 * c:
                        continue
                    for pr in range(a.pairs):
                        e = g * a.pairs + pr
                        pool.wait_ge(s["exp"].sem, s["exp"].at(b, e + 1))
                        p = probs[:, e % 6, :, 0:P]
                        G.affine_select(out=p, in_=p, compare_op=ALU.is_ge, fill=0.0, base=0,
                                        pattern=[[0, 2], [1, P]], channel_multiplier=-1
                                        ).then_inc(s["masked"].sem, 1)

            for b in range(BATCH):
                chain(b, items[0])
                attention(b, QKV0)
                chain(b, items[1])
                attention(b, QKV1)
                chain(b, items[2])


_INS = ["L0_attn_x", "L0_attn_w_qkv", "L0_attn_b_qkv", "L0_attn_w_o", "L0_attn_b_o", "L0_ffn_W", "L0_ffn_lora_A",
        "L0_ffn_lora_B", "L0_ffn_magnitude", "L1_attn_w_qkv", "L1_attn_b_qkv", "L1_attn_w_o", "L1_attn_b_o",
        "L1_ffn_W_base", "L1_ffn_b_base", "L1_ffn_W_router", "L1_ffn_lora_A", "L1_ffn_lora_B"]


def kernel(**inputs):
    import concourse.bacc as bacc
    from concourse.bass_utils import run_bass_kernel_spmd

    a = {n: np.asarray(inputs[n]) for n in _INS}
    lora_a = a["L1_ffn_lora_A"].reshape(ER, D)
    inv_freq = (1.0 / np.float32(10000.0) ** (np.arange(0, 16, 2, dtype=np.float32) / np.float32(16))).astype(np.float32)
    angle = np.arange(SEQ, dtype=np.float32)[:, None] * inv_freq[None, :]
    cos, sin = np.cos(angle).astype(np.float32), np.sin(angle).astype(np.float32)
    arrays = {
        "x": a["L0_attn_x"],
        "rope_cos": np.repeat(cos, 2, axis=1),
        "rope_sin": np.stack([-sin, sin], axis=-1).reshape(SEQ, 16),
        "ffn_w": a["L0_ffn_W"].T, "ffn_a": a["L0_ffn_lora_A"], "ffn_b": a["L0_ffn_lora_B"].T,
        "mag": a["L0_ffn_magnitude"],
        "wqkv0": a["L0_attn_w_qkv"].T[:, A0.feature_order()], "bqkv0": a["L0_attn_b_qkv"][A0.feature_order()],
        "wo0": a["L0_attn_w_o"].T, "bo0": a["L0_attn_b_o"],
        "wqkv1": a["L1_attn_w_qkv"].T[:, A1.feature_order()], "bqkv1": a["L1_attn_b_qkv"][A1.feature_order()],
        "wo1": a["L1_attn_w_o"].T, "bo1": a["L1_attn_b_o"],
        "base": a["L1_ffn_W_base"].T, "bbase": a["L1_ffn_b_base"],
        "hl": np.concatenate([lora_a, a["L1_ffn_W_router"]], axis=0).T,
        "lora_b": a["L1_ffn_lora_B"].transpose(0, 2, 1).reshape(ER, D),
    }
    arrays = {f"{n}_dram": np.ascontiguousarray(v) for n, v in arrays.items()}
    nc = bacc.Bacc("TRN2", target_bir_lowering=False, num_devices=1)
    w = {n[:-5]: nc.dram_tensor(n, v.shape, F32, kind="ExternalInput").ap() for n, v in arrays.items()}
    out = nc.dram_tensor("out_dram", (BATCH, SEQ, D), F32, kind="ExternalOutput").ap()
    build(nc, w.pop("x"), w.pop("rope_cos"), w.pop("rope_sin"), w, out)
    r = run_bass_kernel_spmd(nc, [arrays], core_ids=[0])
    return r.results[0]["out_dram"]
```

```python
from contextlib import ExitStack

import numpy as np

import concourse.bass as bass
from concourse import mybir

F32 = mybir.dt.float32
F32R = mybir.dt.float32r
BF16 = mybir.dt.bfloat16
U32 = mybir.dt.uint32
ALU = mybir.AluOpType
ACT = mybir.ActivationFunctionType
AX = mybir.AxisListType

P = 128
BATCH, SEQ, D = 2, 1024, 512
NT = SEQ // P
KC = D // P
HALF = 512
EPS = 1e-5
EXPERTS, RANK = 8, 16
ER = EXPERTS * RANK
NEG = -1e30
SHIFT_DELAY = 3


class Attention:

    def __init__(self, name, q_heads, kv_heads, dim, scale, unit_heads, rope, ahead, slack):
        self.name, self.dim, self.scale, self.rope = name, dim, scale, rope
        self.unit_heads = unit_heads
        self.ahead = ahead
        self.slack = slack
        self.units = q_heads // unit_heads
        self.kv_heads = kv_heads
        self.grouped = q_heads != kv_heads
        self.q_feats, self.kv_feats = q_heads * dim, kv_heads * dim
        self.qk_feats = self.q_feats + self.kv_feats
        self.feats = self.qk_feats + self.kv_feats
        self.blocks = self.qk_feats // P
        self.rows = P // unit_heads
        self.k_copies = 1 if self.grouped else unit_heads
        self.pairs = unit_heads // 2
        self.lag = 2 if self.pairs == 2 else 3
        self.chunks = 2 * self.units
        self.steps = [(c, j, max(HALF * c, P * j), HALF * (c + 1) - max(HALF * c, P * j))
                      for c in range(2) for j in range(4 * c + 4)]
        self.last_step = [3, len(self.steps) - 1]
        six = [(1, 1), (1, 2), (2, 1), (2, 2), (1, 3), (3, 1)]
        self.main_parts = six if dim == 16 else six[:3]
        self.rest_parts = [] if dim == 16 else six[3:]
        self.main_loads, self.rest_loads = self.loads(self.main_parts), self.loads(self.rest_parts)
        self.max_chunks = []
        for t in range(NT):
            for kp in range(1 + (t >= 4)):
                w = P * (t + 1) - HALF * kp if kp or t < 4 else HALF
                n = min(HALF // w, unit_heads)
                self.max_chunks += [(t, kp, w, h, n) for h in range(0, unit_heads, n)]
        self.max_chunks_of = [sum(ch[0] < 4 for ch in self.max_chunks), len(self.max_chunks)]
        self.begun = {5: 0, 6: 3, 7: self.max_chunks_of[0]}
        self.slots = 3
        self.plan_ring()

    def loads(self, rows):
        nq, nk = self.unit_heads, self.k_copies
        out = []
        for i, (pq, pk) in enumerate(rows):
            out += [(i, pq, 0, nq + nk)] if pq == pk else [(i, pq, 0, nq), (i, pk, nq, nk)]
        return out

    def feature_order(self):
        def blocks(first, heads):
            f = first + np.arange(heads * self.units * self.dim).reshape(self.units, heads, self.dim)
            return f.transpose(1, 0, 2).reshape(-1)
        return np.concatenate([blocks(0, self.unit_heads), blocks(self.q_feats, self.k_copies),
                               np.arange(self.qk_feats, self.feats)])

    def plan_ring(self):
        ns = len(self.steps)
        total = self.units * ns
        chunks = [(u, n) for u in range(self.units) for n in range(len(self.max_chunks))]
        per = len(self.max_chunks)
        start = self.max_chunks_of[0] + SHIFT_DELAY + self.slack
        catch_up = sum(s[3] for s in self.steps[:3]) / sum(s[3] for s in self.steps)

        def wanted(units_done):
            behind = max(0, 1 - units_done / catch_up) * (per * self.ahead - start)
            return int(per * (self.ahead + units_done) - behind)
        self.ring_at = [[[] for _ in range(self.slots)] for _ in range(total + self.lag + 4)]
        self.ring_first = []
        width = [s[3] for s in self.steps]
        done, due_m = 0, []

        def push(dst, upto):
            nonlocal done
            while done < min(upto, len(chunks)):
                u, n = chunks[done]
                dst.append(("max", u, n))
                for x in due_m:
                    x[1] -= 1
                while due_m and due_m[0][1] <= 0:
                    dst.append(("shift", *due_m.pop(0)[0]))
                if n + 1 in self.max_chunks_of:
                    due_m.append([(u, self.max_chunks_of.index(n + 1)), SHIFT_DELAY])
                done += 1

        push(self.ring_first, start)
        for s in range(total + self.lag + 4):
            for slot in range(self.slots):
                dst = self.ring_at[s][slot]
                if s < total:
                    u, k = divmod(s, ns)
                    share = (sum(width[:k]) + width[k] * (slot + 1) / self.slots) / sum(width)
                    push(dst, wanted(u + share))
                    if done == len(chunks):
                        while due_m:
                            dst.append(("shift", *due_m.pop(0)[0]))
                if slot == 0:
                    for c in range(2):
                        e = s - self.lag - 2 - self.last_step[c]
                        if e >= 0 and e % ns == 0 and e // ns < self.units:
                            dst.append(("norm", e // ns, c))
        self.ring = self.ring_first + [x for step in self.ring_at for slot in step for x in slot]
        self.ring_len = len(self.ring)
        self.norm_at = [i for i, item in enumerate(self.ring) if item[0] == "norm"]


A0 = Attention("rot", 32, 8, 16, 0.25, 4, True, ahead=1.07, slack=12)
A1 = Attention("std", 8, 8, 32, 1.0, 2, False, ahead=1.07, slack=12)

FFN_A, QKV0, WO0, FFN_B, MOE_A, QKV1, WO1, MOE_B = range(8)
LN_RANK = {FFN_A: 0, QKV0: 1, FFN_B: 2, MOE_A: 3, QKV1: 4, MOE_B: 5}
UPD_RANK = {FFN_A: 0, WO0: 1, FFN_B: 2, MOE_A: 3, WO1: 4, MOE_B: 5}
BIAS_RANK = {WO0: 0, MOE_A: 1, WO1: 2, MOE_B: 3}
MOE_RANK = {MOE_A: 0, MOE_B: 1}
CHAINS = [[FFN_A, QKV0], [WO0, FFN_B, MOE_A, QKV1], [WO1, MOE_B]]
ATT = {QKV0: A0, QKV1: A1}
WO_ATT = {WO0: A0, WO1: A1}


class Signal:

    def __init__(self, nc, ctx, name, per_seq):
        self.sem = ctx.enter_context(nc.semaphore(name))
        self.per_seq = per_seq

    def at(self, b, n):
        return b * self.per_seq + n


def build(nc, x_in, rope_cos, rope_sin, W, scratch, out):
    ctx = ExitStack()
    with ctx:
        def sb(name, shape, dt=F32):
            return ctx.enter_context(nc.sbuf_tensor(name, shape, dt))

        def signal(name, per_seq):
            return Signal(nc, ctx, name, per_seq)

        def wait(eng, sig, b, n):
            if b > 0 or n > 0:
                eng.wait_ge(sig.sem, sig.at(b, n))

        x = sb("x", [P, NT, D])
        features = sb("features", [P, KC * SEQ])
        xT = sb("xT", [P, 2, 2, KC, P], F32R)
        qkT_mem = sb("qkT_mem", [P, 5 * 3 * SEQ], BF16)
        v_mem = sb("v_mem", [P, NT * 8 * 33])
        probs = sb("probs", [P, 6, 2, HALF])
        aug_mem = sb("aug_mem", [P, 20480], BF16)
        w_hi = [sb("w_hi_even", [P, KC * D], F32R), sb("w_hi_odd", [P, KC * 768], F32R)]
        w_lo = [sb("w_lo_even", [P, KC * D], F32R), sb("w_lo_odd", [P, KC * 768], F32R)]
        whl = sb("whl", [P, 2, KC, ER + EXPERTS], F32R)
        wlora = sb("wlora", [P, D])
        bqkv = sb("bqkv", [P, 768])
        bx = {WO0: sb("bo0", [P, D]), WO1: sb("bo1", [P, D]), MOE_A: sb("bbase", [P, D])}
        bx[MOE_B] = bx[MOE_A]
        cos2 = sb("cos2", [P, NT, 16])
        sin2 = sb("sin2", [P, NT, 16])
        identf = sb("identf", [P, P])
        identb = sb("identb", [P, P], BF16)
        causal = sb("causal", [P, P], BF16)
        expert_no = sb("expert_no", [P, EXPERTS])
        minus_half = sb("minus_half", [P, 1])
        stats = sb("stats", [P, 2, 6])
        mv = sb("mv", [P, 3, 2])
        var_eps = sb("var_eps", [P, 3, 1])
        rstd = sb("rstd", [P, 3, 1])
        top = sb("top", [P, 8])
        top_at = sb("top_at", [P, 8], U32)
        top_atf = sb("top_atf", [P, 2])
        route = sb("route", [P, 8])
        gate = sb("gate", [P, 2, EXPERTS])
        maxes = sb("maxes", [P, 2, 2, 4, NT])
        shifts = sb("shifts", [P, 2, 64], BF16)
        shiftT = sb("shiftT", [32, 2, P], BF16)
        heads_raw = sb("heads_raw", [P, 2, HALF])
        hw_mem = sb("hw_mem", [P, 4, P])
        hw = [hw_mem[:, i, :] for i in range(2)]
        hwT = [hw_mem[:, 2 + i, :] for i in range(2)]
        inv_sum = sb("inv_sum", [P, 16])

        work = aug_mem[:, :].bitcast(F32)
        at = [0]

        def carve(n):
            at[0] += n
            return work[:, at[0] - n:at[0]]
        xn = [carve(D) for _ in range(2)]
        qkv = [carve(768) for _ in range(3)]
        rot = [carve(640) for _ in range(2)]
        rc = carve(640)
        rs = carve(640)
        rest = [carve(640) for _ in range(2)]
        parts = [carve(960).bitcast(BF16).rearrange("p (n f) -> p n f", n=3) for _ in range(3)]
        assert at[0] <= 10240
        eff_mem = work[:, 5120:5120 + KC * D]
        eff = eff_mem.rearrange("p (k n) -> p k n", k=KC)
        whl_raw = work[:, 2048:2048 + KC * (ER + EXPERTS)].rearrange("p (k n) -> p k n", k=KC)
        ones = work[:, 2600:2728]
        dora_a = work[0:32, 2728:3240]
        dora_b = work[0:32, 3240:3752]
        magnitude = work[:, 3752:4264]

        def weights(st, part):
            n = ATT[st].feats if st in ATT else D
            kc = 2 if st == WO1 else KC
            return part[st % 2][:, 0:kc * n].rearrange("p (k n) -> p k n", k=kc)

        def aug_main(a, u):
            if a is A0:
                return aug_mem[:, 5120 * (u % 3):5120 * (u % 3) + 5120].rearrange("p (c n s) -> p c n s", c=2, n=5)
            return aug_mem[:, 4096 * (u % 3):4096 * (u % 3) + 4096].rearrange("p (c n s) -> p c n s", c=2, n=4)

        def aug_rest(u):
            return aug_mem[:, 12288 + 4096 * (u % 2):16384 + 4096 * (u % 2)].rearrange("p (c n s) -> p c n s", c=2, n=4)

        def q_and_k(a, operands):
            return operands[:, :, 0:a.unit_heads, :], operands[:, :, a.unit_heads:, :]

        def values(a):
            w = a.dim + 1
            return v_mem[:, 0:NT * 8 * w].rearrange("p (t h w) -> p t h w", t=NT, h=8)

        def aug_early(a):
            n = a.unit_heads + a.k_copies
            return features[:, 0:n * HALF // 2].bitcast(BF16).rearrange("p (n s) -> p n s", n=n).unsqueeze(1)

        def qkT(a):
            return qkT_mem[:, 0:a.blocks * 3 * SEQ].rearrange("p (c n s) -> p c n s", c=2, s=HALF)

        bank = ctx.enter_context(nc.psum_tensor("bank", [P, 8, 512], F32))
        turn = [bank[:, 0, :], bank[:, 1, :]]
        prod = [bank[:, 2:4, :], bank[:, 4:6, :]]
        prod_flat = [p.rearrange("p n c -> p (n c)") for p in prod]
        partT_at = [bank[:, n:n + 2, :].bitcast(BF16).rearrange("p n (b c) -> p (n b) c", c=P) for n in (6, 0)]
        partT = [partT_at[t > 4] for t in range(NT)]
        scores = bank[:, 0:4, :]
        ring = [bank[:, 4, :], bank[:, 5, :], bank[:, 7, :]]
        heads = bank[:, 6, :]

        s_const = signal("const_ready", 0)
        s_pool = signal("pool_memsets", 0)
        gate_sum = signal("gate_sum", 2 * NT)
        staged = {n: ctx.enter_context(nc.semaphore(f"staged_{n}")) for n in ("wqkv0", "wo0", "base", "wqkv1", "wo1")}
        s_early = ctx.enter_context(nc.semaphore("tables_loaded"))
        s_w = ctx.enter_context(nc.semaphore("biases_loaded"))
        s_scratch = ctx.enter_context(nc.semaphore("dora_weight_stored"))
        s_ffn_in = ctx.enter_context(nc.semaphore("ffn_inputs_loaded"))
        s_eff = {n: ctx.enter_context(nc.semaphore(f"eff_{n}")) for n in
                 ("ab", "sum", "sq", "norm", "sqrt", "inv", "scale", "ready", "half_bias", "router_parts")}
        w_loaded = [signal(f"w_loaded{i}", 16 * 4) for i in range(2)]
        bqkv_loaded = signal("bqkv_loaded", 32)
        chunks_of = [2 if st == WO1 else KC for st in range(8)]
        w_hi_ready = signal("w_hi_ready", sum(chunks_of))
        w_ready = signal("w_ready", sum(chunks_of))

        def chunks_before(st):
            return sum(chunks_of[:st])
        x_loaded = [signal(f"x_loaded{t}", 16) for t in range(NT)]
        x_stored = [signal(f"x_stored{t}", 16) for t in range(NT)]
        ln_stat = signal("ln_stat", 6 * NT)
        ln_mv = signal("ln_mv", 6 * NT)
        ln_eps = signal("ln_eps", 6 * NT)
        ln_rstd = signal("ln_rstd", 6 * NT)
        xn_ready = signal("xn_ready", 6 * NT)
        turned = signal("turned", 8 * NT)
        xT_hi_ready = signal("xT_hi_ready", 8 * NT)
        xT_ready = signal("xT_ready", 8 * NT)
        prod_ready = signal("prod_ready", 8 * NT)
        x_new = signal("x_new", 6 * NT)
        x_biased = signal("x_biased", 4 * NT)
        hl_ready = signal("hl_ready", 2 * NT)
        route_step = signal("route_step", 2 * NT * 9)
        route_exp = signal("route_exp", 2 * NT)
        hw_ready = signal("hw_ready", 2 * NT)
        hw_turned = signal("hw_turned", 2 * NT)
        hwT_ready = signal("hwT_ready", 2 * NT)
        qs = {}
        for st, a in ATT.items():
            n = a.name
            s = {}
            s["qkv"] = signal(f"{n}_qkv_ready", NT)
            s["roped"] = signal(f"{n}_roped", NT)
            s["cos"] = signal(f"{n}_cos_product", NT)
            s["sin"] = signal(f"{n}_sin_product", NT)
            s["p1"] = signal(f"{n}_part1", NT)
            s["r1"] = signal(f"{n}_rest1", NT)
            s["p2"] = signal(f"{n}_part2", NT)
            s["p3"] = signal(f"{n}_part3", NT)
            s["v_ones"] = signal(f"{n}_v_ones", 1)
            s["v"] = signal(f"{n}_v_ready", NT)
            s["partT"] = signal(f"{n}_parts_turned", NT)
            s["evA"] = signal(f"{n}_partsT_ready", NT)
            a.main_dmas, a.rest_dmas = len(a.main_loads), len(a.rest_loads)
            s["main"] = [signal(f"{n}_operands{i}", 16 * a.main_dmas * len(range(i, a.units, 3))) for i in range(3)]
            s["early"] = signal(f"{n}_early_operands", 16 * a.main_dmas)
            s["rest"] = [signal(f"{n}_rest_operands{i}", 16 * a.rest_dmas * len(range(i, a.units, 2))) for i in range(2)]
            s["ones"] = signal(f"{n}_one_rows", 1)
            s["shift_rows"] = [signal(f"{n}_shift_rows{i}", 32 * a.units) for i in range(2)]
            s["ring_full"] = signal(f"{n}_ring_full", a.ring_len)
            s["max_done"] = signal(f"{n}_max_done", a.units * len(a.max_chunks))
            s["shift_step"] = signal(f"{n}_shift_step", 3 * a.units)
            s["shift"] = signal(f"{n}_shift_ready", a.chunks)
            s["shiftT"] = signal(f"{n}_shiftT_ready", a.chunks)
            ne = a.units * len(a.steps) * a.pairs
            s["scored"] = signal(f"{n}_scores_ready", ne)
            s["exp"] = signal(f"{n}_exp_done", ne)
            s["masked"] = signal(f"{n}_masked", a.units * 8 * a.pairs)
            s["pv"] = signal(f"{n}_values_done", a.units * len(a.steps))
            s["raw"] = signal(f"{n}_heads_raw", a.chunks)
            s["inv"] = signal(f"{n}_inverse_sum", a.chunks)
            s["normed"] = signal(f"{n}_heads_ready", a.chunks)
            qs[st] = s

        def normed(st, b, eng):
            eng.wait_ge(qs[st]["normed"].sem, qs[st]["normed"].at(b, ATT[st].chunks))

        block = ctx.enter_context(nc.Block())
        items = [[(st, t) for st in chain for t in range(NT)] for chain in CHAINS]

        @block.sync
        def _(sp):
            sp.dma_start(dora_a, W["ffn_a"]).then_inc(s_ffn_in, 16)
            sp.dma_start(dora_b, W["ffn_b"]).then_inc(s_ffn_in, 16)
            sp.dma_start(eff, W["ffn_w"].rearrange("(k p) n -> p k n", p=P)).then_inc(s_ffn_in, 16)
            sp.dma_start(magnitude, W["mag"].partition_broadcast(P)).then_inc(s_ffn_in, 16)

            def load_x(b):
                for t in range(NT):
                    wait(sp, x_stored[t], b, 0)
                    sp.dma_start(x[:, t, :], x_in[b, t * P:(t + 1) * P, :]).then_inc(x_loaded[t].sem, 16)

            def store_x(b):
                for t in range(NT):
                    sp.wait_ge(x_new.sem, x_new.at(b, UPD_RANK[MOE_B] * NT + t + 1))
                    sp.dma_start(out[b, t * P:(t + 1) * P, :], x[:, t, :]).then_inc(x_stored[t].sem, 16)

            def load_tables():
                sp.dma_start(cos2[:, :, :], rope_cos.rearrange("(t p) c -> p t c", p=P)).then_inc(s_early, 16)
                sp.dma_start(sin2[:, :, :], rope_sin.rearrange("(t p) c -> p t c", p=P)).then_inc(s_early, 16)
                sp.dma_start(whl_raw, W["hl"].rearrange("(k p) n -> p k n", p=P)).then_inc(s_early, 16)

            def load_biases():
                for dst, src in ((bx[WO0], W["bo0"]), (bx[WO1], W["bo1"]), (bx[MOE_A], W["bbase"])):
                    sp.dma_start(dst[:, :], src.partition_broadcast(P)).then_inc(s_w, 16)
                sp.dma_start(wlora[:, :], W["lora_b"]).then_inc(s_w, 16)

            def load_weights(b, st):
                wait(sp, prod_ready, b, (st - 1) * NT)
                name = {QKV0: "wqkv0", QKV1: "wqkv1", WO0: "wo0", WO1: "wo1", MOE_A: "base", MOE_B: "base"}.get(st, "dora")
                if name in staged:
                    sp.wait_ge(staged[name], 16)
                sp.dma_start(weights(st, w_lo).bitcast(F32), scratch[name].rearrange("(k p) n -> p k n", p=P)
                             ).then_inc(w_loaded[st % 2].sem, 16)
                if st in ATT:
                    sp.dma_start(bqkv[:, :], W["bqkv0" if st == QKV0 else "bqkv1"].partition_broadcast(P)
                                 ).then_inc(bqkv_loaded.sem, 16)

            def chain(b, layers):
                for st in layers:
                    if st < MOE_B:
                        load_weights(b, st + 1)
                    elif b + 1 < BATCH:
                        load_weights(b + 1, FFN_A)

            def load_parts(a, dst, loads, u, sem):
                src = qkT(a)[:, 0:dst.shape[1], :, :]
                f = u * a.dim
                for i, part, first, n in loads:
                    at = (part - 1) * a.blocks + first
                    sp.dma_start(dst[a.dim * i:a.dim * (i + 1), :, first:first + n, :],
                                 src[f:f + a.dim, :, at:at + n, :]).then_inc(sem, 16)

            def load_operands(b, st, u):
                a, s = ATT[st], qs[st]
                if u >= 3:
                    sp.wait_ge(s["pv"].sem, s["pv"].at(b, (u - 2) * len(a.steps)))
                load_parts(a, aug_main(a, u), a.main_loads, u, s["main"][u % 3].sem)

            def load_rest(b, st, u):
                a, s = ATT[st], qs[st]
                if u >= 2:
                    sp.wait_ge(s["pv"].sem, s["pv"].at(b, (u - 1) * len(a.steps)))
                load_parts(a, aug_rest(u), a.rest_loads, u, s["rest"][u % 2].sem)

            def load_shifts(b, st, u, c):
                a, s = ATT[st], qs[st]
                q, _ = q_and_k(a, aug_main(a, u))
                n = 4 * a.unit_heads
                sp.wait_ge(s["shiftT"].sem, s["shiftT"].at(b, 2 * u + c + 1))
                for part in range(2):
                    sp.dma_start(q[96 + part:97 + part, c, :, :].rearrange("o h (t s) -> o (h t) s", s=P),
                                 shiftT[part * n:(part + 1) * n, c, :]).then_inc(s["shift_rows"][c].sem, 16)

            def attention(b, st):
                a, s = ATT[st], qs[st]
                sp.wait_ge(s["evA"].sem, s["evA"].at(b, 4))
                load_parts(a, aug_early(a), a.main_loads, 0, s["early"].sem)
                sp.wait_ge(s["evA"].sem, s["evA"].at(b, NT))
                for u in range(3):
                    load_operands(b, st, u)
                    if a.rest_parts and u < 2:
                        load_rest(b, st, u)
                    if u < 2:
                        load_shifts(b, st, 0, u)
                for u in range(a.units):
                    if u + 1 < a.units:
                        load_shifts(b, st, u + 1, 0)
                        load_shifts(b, st, u + 1, 1)
                    if u + 3 < a.units:
                        load_operands(b, st, u + 3)
                    if a.rest_parts and u + 2 < a.units:
                        load_rest(b, st, u + 2)

            def stage(name):
                sp.dma_start(scratch[name], W[name]).then_inc(staged[name], 16)

            load_x(0)
            load_tables()
            for name in staged:
                stage(name)
            sp.wait_ge(s_eff["ready"], KC)
            sp.dma_start(scratch["dora"].rearrange("(k p) n -> p k n", p=P), eff).then_inc(s_scratch, 16)
            sp.wait_ge(s_scratch, 16)
            for b in range(BATCH):
                chain(b, CHAINS[0])
                if b == 0:
                    load_biases()
                attention(b, QKV0)
                chain(b, CHAINS[1])
                attention(b, QKV1)
                chain(b, CHAINS[2])
                store_x(b)
                if b + 1 < BATCH:
                    load_x(b + 1)
            for t in range(NT):
                sp.wait_ge(x_stored[t].sem, x_stored[t].at(BATCH, 0))

        @block.tensor
        def _(pe):
            mm = nc.tensor.matmul
            pe.wait_ge(s_ffn_in, 64)
            pe.wait_ge(s_const.sem, 7)
            for k in range(KC):
                mm(bank[:, k, :], dora_a[:, k * P:(k + 1) * P], dora_b, start=True, stop=True
                   ).then_inc(s_eff["ab"], 1)
            for k in range(KC):
                pe.wait_ge(s_eff["sq"], k + 1)
                last = mm(bank[:, 4, :], ones, probs[:, k, 0, :], start=(k == 0), stop=(k == KC - 1))
            last.then_inc(s_eff["norm"], 1)

            def turn_x(b, st, t):
                n = st * NT + t
                if st in WO_ATT:
                    if t == 0:
                        normed(QKV0 if st == WO0 else QKV1, b, pe)
                    src = features[:, t * D:(t + 1) * D]
                    kc = KC if st == WO0 else 2
                else:
                    pe.wait_ge(xn_ready.sem, xn_ready.at(b, LN_RANK[st] * NT + t + 1))
                    src, kc = xn[n % 2], KC
                wait(pe, xT_ready, b, n - 1)
                for k in range(kc):
                    last = nc.tensor.transpose(turn[n % 2][:, k * P:(k + 1) * P], src[:, k * P:(k + 1) * P], identf[:])
                last.then_inc(turned.sem, 1)

            def begin(b, st, t):
                n = st * NT + t
                pe.wait_ge(xT_ready.sem, xT_ready.at(b, n + 1))
                if n >= 2:
                    st2, t2 = divmod(n - 2, NT)
                    read, m = (qs[st2]["qkv"], t2 + 1) if st2 in ATT else (x_new, UPD_RANK[st2] * NT + t2 + 1)
                    wait(pe, read, b, m)
                else:
                    wait(pe, x_new, b, n - 1)
                return n

            def three_passes(dst, n, hi, lo, lora=False):
                x_hi, x_lo = xT[:, n % 2, 0, :, :], xT[:, n % 2, 1, :, :]
                kc = hi.shape[1]
                for k in range(kc):
                    mm(dst, x_hi[:, k, :], hi[:, k, :], start=(k == 0), stop=False)
                    mm(dst, x_hi[:, k, :], lo[:, k, :], start=False, stop=False)
                    last = mm(dst, x_lo[:, k, :], hi[:, k, :], start=False, stop=(k == kc - 1 and not lora))
                return last

            def product(b, st, t):
                n = st * NT + t
                if st not in MOE_RANK:
                    begin(b, st, t)
                if t == 0:
                    pe.wait_ge(w_ready.sem, w_ready.at(b, chunks_before(st + 1)))
                hi, lo = weights(st, w_hi), weights(st, w_lo)
                for c in range(2 if st in ATT else 1):
                    cols = slice(c * 512, min(hi.shape[2], (c + 1) * 512))
                    last = three_passes(prod[n % 2][:, c, 0:cols.stop - cols.start], n, hi[:, :, cols], lo[:, :, cols],
                                        lora=st in MOE_RANK)
                if st not in MOE_RANK:
                    last.then_inc(prod_ready.sem, 1)

            def router(b, st, t):
                n = begin(b, st, t)
                three_passes(prod[n % 2][:, 1, 0:ER + EXPERTS], n, whl[:, 0, :, :], whl[:, 1, :, :]
                             ).then_inc(hl_ready.sem, 1)

            def turn_hw(b, st, t):
                n, r = st * NT + t, MOE_RANK[st] * NT + t
                pe.wait_ge(hw_ready.sem, hw_ready.at(b, r + 1))
                nc.tensor.transpose(prod[n % 2][:, 1, 256:256 + P], hw[r % 2], identf[:]).then_inc(hw_turned.sem, 1)

            def lora(b, st, t):
                n, r = st * NT + t, MOE_RANK[st] * NT + t
                pe.wait_ge(hwT_ready.sem, hwT_ready.at(b, r + 1))
                mm(prod[n % 2][:, 0, :], hwT[r % 2], wlora[:, :], start=False, stop=True).then_inc(prod_ready.sem, 1)

            def turn_parts(b, st, t):
                a, s = ATT[st], qs[st]
                pe.wait_ge(s["p3"].sem, s["p3"].at(b, t + 1))
                if t > 0:
                    pe.wait_ge(s["evA"].sem, s["evA"].at(b, t))
                for m in range(3):
                    for f in range(a.blocks):
                        last = nc.tensor.transpose(partT[t][:, m * a.blocks + f, :], parts[t % 3][:, m, f * P:(f + 1) * P],
                                                   identb[:])
                last.then_inc(s["partT"].sem, 1)

            def ring_item(b, st, i):
                a, s = ATT[st], qs[st]
                kind, u, n = a.ring[i]
                dst = ring[i % 3]
                if i >= 3:
                    ring_free(b, st, i)
                if kind == "max":
                    t, kp, w, h0, nh = a.max_chunks[n]
                    early = u == 0 and t < 4
                    q, k = q_and_k(a, aug_early(a) if early else aug_main(a, u))
                    if early and n == 0:
                        pe.wait_ge(s["early"].sem, s["early"].at(b, 16 * a.main_dmas))
                    elif n == (a.max_chunks_of[0] if u == 0 else 0):
                        m = s["main"][u % 3]
                        pe.wait_ge(m.sem, m.at(b, 16 * a.main_dmas * (u // 3 + 1)))
                    diag = kp == 1 or t < 4
                    for h in range(nh):
                        last = mm(dst[:, h * w:(h + 1) * w], q[0:96, t // 4, h0 + h, t % 4 * P:(t % 4 + 1) * P],
                                  k[0:96, kp, (h0 + h) % a.k_copies, 0:w],
                                  start=True, stop=not diag)
                        if diag:
                            last = mm(dst[:, (h + 1) * w - P:(h + 1) * w], identb[:], causal[:],
                                      start=False, stop=True)
                elif kind == "shift":
                    m = 8 * a.unit_heads
                    pe.wait_ge(s["shift"].sem, s["shift"].at(b, 2 * u + n + 1))
                    last = nc.tensor.transpose(dst[0:m, 0:P // 2].bitcast(BF16), shifts[:, n, 0:m], identb[:])
                else:
                    c = 2 * u + n
                    pe.wait_ge(s["raw"].sem, s["raw"].at(b, c + 1))
                    for j in range(4):
                        last = nc.tensor.transpose(dst[:, j * P:(j + 1) * P],
                                                   heads_raw[:, c % 2, j * P:(j + 1) * P], identf[:])
                last.then_inc(s["ring_full"].sem, 1)

            def ring_free(b, st, i):
                a, s = ATT[st], qs[st]
                kind, u, n = a.ring[i - 3]
                read, m = {"max": (s["max_done"], u * len(a.max_chunks) + n + 1), "shift": (s["shiftT"], 2 * u + n + 1),
                           "norm": (s["normed"], 2 * u + n + 1)}[kind]
                pe.wait_ge(read.sem, read.at(b, m))

            def chain(b, its):
                for i in range(len(its) + 6):
                    if i < len(its):
                        turn_x(b, *its[i])
                    if 2 <= i < len(its) + 2 and its[i - 2][0] in MOE_RANK:
                        turn_hw(b, *its[i - 2])
                    if 1 <= i < len(its) + 1 and its[i - 1][0] in MOE_RANK:
                        router(b, *its[i - 1])
                    if 2 <= i < len(its) + 2 and its[i - 2][0] in MOE_RANK:
                        lora(b, *its[i - 2])
                    if 1 <= i < len(its) + 1:
                        product(b, *its[i - 1])
                    if 5 <= i < len(its) + 5 and its[i - 5][0] in ATT:
                        st, t = its[i - 5]
                        turn_parts(b, st, t)
                        for n in range(ATT[st].begun.get(t - 1, 0), ATT[st].begun.get(t, 0)):
                            ring_item(b, st, n)

            def attention(b, st):
                a, s = ATT[st], qs[st]
                ns = len(a.steps)
                v = values(a)
                count = {"ring": a.begun[NT - 1], "diag": 0}

                def ring_items(n):
                    for i in range(count["ring"], count["ring"] + n):
                        ring_item(b, st, i)
                    count["ring"] += n

                def score(g, first, last_):
                    u, k_ = divmod(g, ns)
                    c, j, q0, w = a.steps[k_]
                    q, k = q_and_k(a, aug_main(a, u))
                    if j == 0 and first == 0:
                        sr = s["shift_rows"][c]
                        pe.wait_ge(sr.sem, sr.at(b, 32 * (u + 1)))
                        if a.rest_parts and c == 0:
                            m = s["rest"][u % 2]
                            pe.wait_ge(m.sem, m.at(b, 16 * a.rest_dmas * (u // 2 + 1)))
                    for h in range(first, last_):
                        e = g * a.pairs + h // 2
                        if e >= 2 and h % 2 == 0:
                            pe.wait_ge(s["exp"].sem, s["exp"].at(b, e - 1))
                        dst = scores[:, 2 * (e % 2) + h % 2, 0:w]
                        keys, queries = slice(j % 4 * P, (j % 4 + 1) * P), slice(q0 - HALF * c, HALF)
                        last = mm(dst, k[0:98, j // 4, h % a.k_copies, keys], q[0:98, c, h, queries],
                                  start=True, stop=not a.rest_parts)
                        if a.rest_parts:
                            q2, k2 = q_and_k(a, aug_rest(u))
                            last = mm(dst, k2[0:96, j // 4, h, keys], q2[0:96, c, h, queries],
                                      start=False, stop=True)
                        if h % 2 == 1:
                            last.then_inc(s["scored"].sem, 1)

                def value(g):
                    u, k_ = divmod(g, ns)
                    c, j, q0, w = a.steps[k_]
                    ch = 2 * u + c
                    e = g * a.pairs
                    if j >= 4 * c:
                        count["diag"] += a.pairs
                        pe.wait_ge(s["masked"].sem, s["masked"].at(b, count["diag"]))
                    pe.wait_ge(s["exp"].sem, s["exp"].at(b, e + a.pairs))
                    if j == 0 and ch >= 1:
                        pe.wait_ge(s["raw"].sem, s["raw"].at(b, ch))
                    for h in range(a.unit_heads):
                        kv = u if a.grouped else u * a.unit_heads + h
                        last = mm(heads[a.rows * h:a.rows * h + a.dim + 1, q0 - HALF * c:HALF],
                                  v[:, j, kv, :], probs[:, (e + h // 2) % 6, h % 2, 0:w],
                                  start=(j == 0), stop=(j == 4 * c + 3))
                    last.then_inc(s["pv"].sem, 1)

                ring_items(len(a.ring_first) - count["ring"])
                pe.wait_ge(s["ones"].sem, s["ones"].at(b, 1))
                pe.wait_ge(s["v_ones"].sem, s["v_ones"].at(b, 1))
                pe.wait_ge(s["v"].sem, s["v"].at(b, NT))
                for g in range(a.units * ns + a.lag + 4):
                    half = a.unit_heads // 2
                    if g < a.units * ns:
                        score(g, 0, half)
                    ring_items(len(a.ring_at[g][0]))
                    if g < a.units * ns:
                        score(g, half, a.unit_heads)
                    ring_items(len(a.ring_at[g][1]))
                    if a.lag <= g < a.units * ns + a.lag:
                        value(g - a.lag)
                    ring_items(len(a.ring_at[g][2]))

            for b in range(BATCH):
                chain(b, items[0])
                attention(b, QKV0)
                pe.wait_ge(s_w, 16 * 4)
                pe.wait_ge(s_eff["router_parts"], 2)
                chain(b, items[1])
                attention(b, QKV1)
                chain(b, items[2])

        @block.vector
        def _(dve):
            V = nc.vector
            def statistics(b, st, t):
                if st not in LN_RANK:
                    return
                l = LN_RANK[st]
                n = l * NT + t
                i = n % 2
                if l == 0:
                    dve.wait_ge(x_loaded[t].sem, x_loaded[t].at(b, 16))
                else:
                    dve.wait_ge(x_new.sem, x_new.at(b, (l - 1) * NT + t + 1))
                V.bn_stats(stats[:, i, :], x[:, t, :]).then_inc(ln_stat.sem, 1)
                dve.wait_ge(ln_stat.sem, ln_stat.at(b, n + 1))
                V.bn_aggr(mv[:, n % 3, :], stats[:, i, :]).then_inc(ln_mv.sem, 1)

            def normalise(b, st, t):
                if st not in LN_RANK:
                    return
                n = LN_RANK[st] * NT + t
                dve.wait_ge(ln_rstd.sem, ln_rstd.at(b, n + 1))
                wait(dve, turned, b, st * NT + t - 1)
                V.tensor_scalar(xn[t % 2], x[:, t, :], mv[:, n % 3, 0:1], rstd[:, n % 3, :],
                                ALU.subtract, ALU.mult).then_inc(xn_ready.sem, 1)

            def turned_lo(b, st, t):
                n = st * NT + t
                kc = chunks_of[st]
                dve.wait_ge(xT_hi_ready.sem, xT_hi_ready.at(b, n + 1))
                V.tensor_tensor(xT[:, n % 2, 1, 0:kc, :], turn[n % 2][:, 0:kc * P].rearrange("p (k c) -> p k c", k=kc),
                                xT[:, n % 2, 0, 0:kc, :].bitcast(F32), ALU.subtract).then_inc(xT_ready.sem, 1)

            def epilogue(b, st, t):
                n = st * NT + t
                dve.wait_ge(prod_ready.sem, prod_ready.at(b, n + 1))
                if st in ATT:
                    a, s = ATT[st], qs[st]
                    if b == 0 and st == QKV0 and t == 0:
                        dve.wait_ge(s_eff["router_parts"], 2)
                        dve.wait_ge(s_scratch, 16)
                    if t == 0:
                        dve.wait_ge(bqkv_loaded.sem, bqkv_loaded.at(b, 16 if st == QKV0 else 32))
                    if t >= 3:
                        dve.wait_ge(s["v"].sem, s["v"].at(b, t - 2))
                        dve.wait_ge(s["roped"].sem if a.rope else s["p1"].sem, s["p1"].at(b, t - 2))
                        if not a.rope:
                            dve.wait_ge(s["r1"].sem, s["r1"].at(b, t - 2))
                    V.tensor_tensor(qkv[t % 3][:, 0:a.feats], prod_flat[n % 2][:, 0:a.feats], bqkv[:, :], ALU.add
                                    ).then_inc(s["qkv"].sem, 1)
                    return
                if st in BIAS_RANK:
                    dve.wait_ge(x_biased.sem, x_biased.at(b, BIAS_RANK[st] * NT + t + 1))
                    scale = 0.5 if st in MOE_RANK else 1.0
                    V.scalar_tensor_tensor(x[:, t, :], prod[n % 2][:, 0, :], scale, x[:, t, :], ALU.mult, ALU.add
                                           ).then_inc(x_new.sem, 1)
                else:
                    V.tensor_tensor(x[:, t, :], prod[n % 2][:, 0, :], x[:, t, :], ALU.add
                                    ).then_inc(x_new.sem, 1)

            def routing(b, st, t):
                n, r = st * NT + t, MOE_RANK[st] * NT + t
                logits = prod[n % 2][:, 1, ER:ER + EXPERTS]
                step = [9 * r]

                def link(ins):
                    step[0] += 1
                    ins.then_inc(route_step.sem, 1)
                    dve.wait_ge(route_step.sem, route_step.at(b, step[0]))
                dve.wait_ge(hl_ready.sem, hl_ready.at(b, r + 1))
                link(V.max(top[:], logits))
                link(V.tensor_tensor(route[:, 0:1], top[:, 1:2], top[:, 0:1], ALU.subtract))
                link(V.max_index(top_at[:], top[:], logits))
                link(V.tensor_copy(top_atf[:], top_at[:, 0:2]))
                dve.wait_ge(route_exp.sem, route_exp.at(b, r + 1))
                link(V.tensor_scalar(route[:, 2:3], route[:, 1:2], 1.0, 0.5, ALU.add, ALU.mult))
                link(V.reciprocal(route[:, 3:4], route[:, 2:3]))
                link(V.tensor_tensor(route[:, 4:5], route[:, 1:2], route[:, 3:4], ALU.mult))
                link(V.tensor_scalar(gate[:, 0, :], expert_no[:], top_atf[:, 0:1], route[:, 3:4], ALU.is_equal, ALU.mult))
                link(V.tensor_scalar(gate[:, 1, :], expert_no[:], top_atf[:, 1:2], route[:, 4:5], ALU.is_equal, ALU.mult))

            def weigh(b, st, t):
                n, r = st * NT + t, MOE_RANK[st] * NT + t
                V.tensor_tensor(gate[:, 0, :], gate[:, 0, :], gate[:, 1, :], ALU.add).then_inc(gate_sum.sem, 1)
                dve.wait_ge(gate_sum.sem, gate_sum.at(b, r + 1))
                wait(dve, hw_turned, b, r - 1)
                V.tensor_tensor(hw[r % 2].rearrange("p (e r) -> p e r", e=EXPERTS),
                                prod[n % 2][:, 1, 0:ER].rearrange("p (e r) -> p e r", e=EXPERTS),
                                gate[:, 0, :].unsqueeze(2).to_broadcast([P, EXPERTS, RANK]), ALU.mult
                                ).then_inc(hw_ready.sem, 1)

            def rope_cos_part(b, st, t):
                a, s = ATT[st], qs[st]
                if a.rope:
                    dve.wait_ge(s["qkv"].sem, s["qkv"].at(b, t + 1))
                    V.tensor_tensor(rc.rearrange("p (h d) -> p h d", d=16),
                                    qkv[t % 3][:, 0:a.qk_feats].rearrange("p (h d) -> p h d", d=16),
                                    cos2[:, t, :].unsqueeze(1).to_broadcast([P, a.qk_feats // 16, 16]), ALU.mult
                                    ).then_inc(s["cos"].sem, 1)

            def rope_sum(b, st, t):
                a, s = ATT[st], qs[st]
                if a.rope:
                    dve.wait_ge(s["cos"].sem, s["cos"].at(b, t + 1))
                    dve.wait_ge(s["sin"].sem, s["sin"].at(b, t + 1))
                    V.tensor_tensor(rot[t % 2], rc, rs, ALU.add).then_inc(s["roped"].sem, 1)

            def rest1(b, st, t):
                a, s = ATT[st], qs[st]
                src = rot[t % 2] if a.rope else qkv[t % 3]
                dve.wait_ge(s["p1"].sem, s["p1"].at(b, t + 1))
                if t >= 2:
                    dve.wait_ge(s["p3"].sem, s["p3"].at(b, t - 1))
                V.tensor_tensor(rest[t % 2][:, 0:a.qk_feats], src[:, 0:a.qk_feats], parts[t % 3][:, 0, 0:a.qk_feats],
                                ALU.subtract).then_inc(s["r1"].sem, 1)

            def begin_chain(b, its):
                statistics(b, *its[0])
                statistics(b, *its[1])
                normalise(b, *its[0])

            def chain(b, its):
                for i in range(len(its) + 4):
                    if i + 2 < len(its):
                        statistics(b, *its[i + 2])
                    if i + 1 < len(its):
                        normalise(b, *its[i + 1])
                    if i < len(its):
                        turned_lo(b, *its[i])
                    if 3 <= i < len(its) + 3 and its[i - 3][0] in ATT:
                        rope_sum(b, *its[i - 3])
                    if 2 <= i < len(its) + 2:
                        epilogue(b, *its[i - 2])
                        if its[i - 2][0] in ATT:
                            rope_cos_part(b, *its[i - 2])
                    if 1 <= i < len(its) + 1 and its[i - 1][0] in MOE_RANK:
                        routing(b, *its[i - 1])
                        weigh(b, *its[i - 1])
                    if 3 <= i < len(its) + 3 and its[i - 3][0] in ATT:
                        rest1(b, *its[i - 3])

            def attention(b, st):
                a, s = ATT[st], qs[st]
                for i, (kind, u, n) in enumerate(a.ring):
                    src = ring[i % 3]
                    dve.wait_ge(s["ring_full"].sem, s["ring_full"].at(b, i + 1))
                    if kind == "max":
                        t, kp, w, h0, nh = a.max_chunks[n]
                        V.tensor_reduce(maxes[:, u % 2, kp, h0:h0 + nh, t],
                                        src[:, 0:nh * w].rearrange("p (h w) -> p h w", h=nh), AX.X, ALU.max
                                        ).then_inc(s["max_done"].sem, 1)
                        if n + 1 in a.max_chunks_of:
                            shift_parts(b, st, u, a.max_chunks_of.index(n + 1))
                    elif kind == "shift":
                        m = 8 * a.unit_heads
                        if u >= 1:
                            sr = s["shift_rows"][n]
                            dve.wait_ge(sr.sem, sr.at(b, 32 * u))
                        V.tensor_copy(shiftT[0:m, n, :], src[0:m, 0:P // 2].bitcast(BF16)
                                      ).then_inc(s["shiftT"].sem, 1)
                    else:
                        c = 2 * u + n
                        nh, d = a.unit_heads, a.dim
                        blocks = src.rearrange("p (g r) -> p g r", r=a.rows)
                        wait(dve, s["normed"], b, c)
                        V.reciprocal(inv_sum[:, 0:4 * nh].unsqueeze(2), blocks[:, :, d:d + 1]).then_inc(s["inv"].sem, 1)
                        dve.wait_ge(s["inv"].sem, s["inv"].at(b, c + 1))
                        width = a.q_feats
                        dst = features[:, :].rearrange("p (t f) -> p t f", f=D)[
                            :, 4 * n:4 * n + 4, u * nh * d:(u + 1) * nh * d].rearrange("p t (h d) -> p t h d", h=nh)
                        V.tensor_tensor(dst, src.rearrange("p (t h r) -> p t h r", t=4, h=nh)[:, :, :, 0:d],
                                        inv_sum[:, 0:4 * nh].rearrange("p (t h) -> p t h", t=4).unsqueeze(3)
                                        .to_broadcast([P, 4, nh, d]), ALU.mult).then_inc(s["normed"].sem, 1)

            def shift_parts(b, st, u, c):
                a, s = ATT[st], qs[st]
                nh, m = a.unit_heads, a.unit_heads * 4
                mx = maxes[:, u % 2, 0, 0:nh, 4 * c:4 * c + 4]
                dve.wait_ge(s["max_done"].sem, s["max_done"].at(b, u * len(a.max_chunks) + a.max_chunks_of[c]))
                if c == 1:
                    V.tensor_tensor(mx, mx, maxes[:, u % 2, 1, 0:nh, 4:8], ALU.max).then_inc(s["shift_step"].sem, 1)
                    dve.wait_ge(s["shift_step"].sem, s["shift_step"].at(b, 3 * u + 2))
                hi = shifts[:, c, 0:m].rearrange("p (h t) -> p h t", h=nh)
                lo = shifts[:, c, m:2 * m].rearrange("p (h t) -> p h t", h=nh)
                V.tensor_scalar(hi, mx, -1.0, None, ALU.mult).then_inc(s["shift_step"].sem, 1)
                dve.wait_ge(s["shift_step"].sem, s["shift_step"].at(b, 3 * u + 1 + 2 * c))
                V.scalar_tensor_tensor(lo, mx, -1.0, hi, ALU.mult, ALU.subtract).then_inc(s["shift"].sem, 1)

            V.memset(minus_half[:], -0.5).then_inc(s_const.sem, 1)
            V.memset(ones, 1.0).then_inc(s_const.sem, 1)
            V.memset(heads, 0.0).then_inc(s_const.sem, 1)
            dve.wait_ge(s_ffn_in, 64)
            for k in range(KC):
                dve.wait_ge(s_eff["ab"], k + 1)
                V.tensor_tensor(eff[:, k, :], bank[:, k, :], eff[:, k, :], ALU.add).then_inc(s_eff["sum"], 1)
            for k in range(KC):
                dve.wait_ge(s_eff["sum"], k + 1)
                V.tensor_tensor(probs[:, k, 0, :], eff[:, k, :], eff[:, k, :], ALU.mult).then_inc(s_eff["sq"], 1)
            begin_chain(0, items[0])
            dve.wait_ge(s_eff["sqrt"], 1)
            V.reciprocal(probs[:, 5, 0, :], probs[:, 4, 0, :]).then_inc(s_eff["inv"], 1)
            dve.wait_ge(s_eff["inv"], 1)
            V.scalar_tensor_tensor(probs[:, 5, 1, :], probs[:, 5, 0, :], 0.5, magnitude, ALU.mult, ALU.mult
                                   ).then_inc(s_eff["scale"], 1)
            dve.wait_ge(s_eff["scale"], 1)
            for k in range(KC):
                V.tensor_tensor(eff[:, k, :], eff[:, k, :], probs[:, 5, 1, :], ALU.mult).then_inc(s_eff["ready"], 1)
            for k in range(KC):
                dve.wait_ge(w_hi_ready.sem, k + 1)
                V.tensor_tensor(weights(FFN_A, w_lo)[:, k, :], eff[:, k, :], weights(FFN_A, w_hi)[:, k, :].bitcast(F32),
                                ALU.subtract).then_inc(w_ready.sem, 1)

            for b in range(BATCH):
                if b > 0:
                    begin_chain(b, items[0])
                chain(b, items[0])
                if b == 0:
                    dve.wait_ge(s_w, 16 * 4)
                    V.tensor_scalar(bx[MOE_A][:, :], bx[MOE_A][:, :], 0.5, None, ALU.mult
                                    ).then_inc(s_eff["half_bias"], 1)
                attention(b, QKV0)
                begin_chain(b, items[1])
                chain(b, items[1])
                attention(b, QKV1)
                begin_chain(b, items[2])
                chain(b, items[2])

        @block.scalar
        def _(act):
            A = nc.scalar
            act.wait_ge(s_early, 16 * 3)
            A.copy(whl[:, 0, :, :], whl_raw).then_inc(s_eff["router_parts"], 1)
            act.wait_ge(s_eff["norm"], 1)
            A.activation(probs[:, 4, 0, :], bank[:, 4, :], ACT.Sqrt).then_inc(s_eff["sqrt"], 1)
            for k in range(KC):
                act.wait_ge(s_eff["ready"], k + 1)
                A.copy(weights(FFN_A, w_hi)[:, k, :], eff[:, k, :]).then_inc(w_hi_ready.sem, 1)

            def copy_turned(b, st, t):
                n = st * NT + t
                kc = chunks_of[st]
                act.wait_ge(turned.sem, turned.at(b, n + 1))
                A.copy(xT[:, n % 2, 0, 0:kc, :], turn[n % 2][:, 0:kc * P].rearrange("p (k c) -> p k c", k=kc)
                       ).then_inc(xT_hi_ready.sem, 1)

            def split_chunk(b, st, k):
                if k == 0:
                    ld = w_loaded[st % 2]
                    act.wait_ge(ld.sem, ld.at(b, 16 * (st // 2 + (st % 2))))
                A.copy(weights(st, w_hi)[:, k, :], weights(st, w_lo)[:, k, :].bitcast(F32)).then_inc(w_hi_ready.sem, 1)

            def gate_exp(b, st, t):
                r = MOE_RANK[st] * NT + t
                act.wait_ge(route_step.sem, route_step.at(b, 9 * r + 2))
                A.activation(route[:, 1:2], route[:, 0:1], ACT.Exp).then_inc(route_exp.sem, 1)

            def copy_hw(b, st, t):
                n, r = st * NT + t, MOE_RANK[st] * NT + t
                act.wait_ge(hw_turned.sem, hw_turned.at(b, r + 1))
                A.copy(hwT[r % 2], prod[n % 2][:, 1, 256:256 + P]).then_inc(hwT_ready.sem, 1)

            def part1(b, st, t):
                a, s = ATT[st], qs[st]
                act.wait_ge(s["roped"].sem if a.rope else s["qkv"].sem, s["qkv"].at(b, t + 1))
                if t >= 3:
                    act.wait_ge(s["partT"].sem, s["partT"].at(b, t - 2))
                src = rot[t % 2] if a.rope else qkv[t % 3]
                A.copy(parts[t % 3][:, 0, 0:a.qk_feats], src[:, 0:a.qk_feats]).then_inc(s["p1"].sem, 1)

            def part2(b, st, t):
                a, s = ATT[st], qs[st]
                act.wait_ge(s["r1"].sem, s["r1"].at(b, t + 1))
                A.copy(parts[t % 3][:, 1, 0:a.qk_feats], rest[t % 2][:, 0:a.qk_feats]).then_inc(s["p2"].sem, 1)

            def evacuate(b, st, t):
                a, s = ATT[st], qs[st]
                act.wait_ge(s["partT"].sem, s["partT"].at(b, t + 1))
                A.copy(qkT(a)[:, t // 4, :, t % 4 * P:(t % 4 + 1) * P], partT[t][:, 0:3 * a.blocks, :]).then_inc(s["evA"].sem, 1)

            def chain(b, its):
                for i in range(len(its) + 7):
                    if i < len(its):
                        copy_turned(b, *its[i])
                        st, t = its[i]
                        nb, nst = (b, st + 1) if st < MOE_B else (b + 1, FFN_A)
                        if nb < BATCH and 2 <= t < 2 + chunks_of[nst]:
                            split_chunk(nb, nst, t - 2)
                    if 2 <= i < len(its) + 2 and its[i - 2][0] in MOE_RANK:
                        copy_hw(b, *its[i - 2])
                    if 6 <= i < len(its) + 6 and its[i - 6][0] in ATT:
                        evacuate(b, *its[i - 6])
                    if 1 <= i < len(its) + 1 and its[i - 1][0] in MOE_RANK:
                        gate_exp(b, *its[i - 1])
                    if 3 <= i < len(its) + 3 and its[i - 3][0] in ATT:
                        part1(b, *its[i - 3])
                    if 4 <= i < len(its) + 4 and its[i - 4][0] in ATT:
                        part2(b, *its[i - 4])

            def attention(b, st):
                a, s = ATT[st], qs[st]
                ns = len(a.steps)
                for g in range(a.units * ns + a.lag + 2):
                    for c in range(2):
                        e = g - a.lag - 1 - a.last_step[c]
                        if e >= 0 and e % ns == 0 and e // ns < a.units:
                            ch = 2 * (e // ns) + c
                            act.wait_ge(s["pv"].sem, s["pv"].at(b, e + a.last_step[c] + 1))
                            if ch >= 2:
                                act.wait_ge(s["ring_full"].sem, s["ring_full"].at(b, a.norm_at[ch - 2] + 1))
                            A.copy(heads_raw[:, ch % 2, :], heads).then_inc(s["raw"].sem, 1)
                    if g < a.units * ns:
                        c, j, q0, w = a.steps[g % ns]
                        for pr in range(a.pairs):
                            e = g * a.pairs + pr
                            act.wait_ge(s["scored"].sem, s["scored"].at(b, e + 1))
                            if e >= 6:
                                act.wait_ge(s["pv"].sem, s["pv"].at(b, (e - 6) // a.pairs + 1))
                            A.activation(probs[:, e % 6, :, 0:w], scores[:, 2 * (e % 2):2 * (e % 2) + 2, 0:w], ACT.Exp,
                                         scale=a.scale).then_inc(s["exp"].sem, 1)

            for b in range(BATCH):
                chain(b, items[0])
                attention(b, QKV0)
                chain(b, items[1])
                attention(b, QKV1)
                chain(b, items[2])

        @block.gpsimd
        def _(pool):
            G = nc.gpsimd

            def mask_tile(tile, fill_first, op, fill, i):
                G.memset(tile[:, :], fill_first).then_inc(s_pool.sem, 1)
                pool.wait_ge(s_pool.sem, i)
                return G.affine_select(out=tile[:, :], in_=tile[:, :], compare_op=op, fill=fill, base=0,
                                       pattern=[[-1, P]], channel_multiplier=1)
            mask_tile(identf, 0.0, ALU.not_equal, 1.0, 1).then_inc(s_const.sem, 1)
            mask_tile(identb, 0.0, ALU.not_equal, 1.0, 2).then_inc(s_const.sem, 1)
            mask_tile(causal, 0.0, ALU.is_ge, NEG, 3).then_inc(s_const.sem, 1)
            G.iota(expert_no[:], pattern=[[1, EXPERTS]], base=0, channel_multiplier=0,
                   allow_small_or_imprecise_dtypes=True).then_inc(s_const.sem, 1)
            pool.wait_ge(s_const.sem, 7)

            def split_chunk(b, st, k):
                n = chunks_before(st) + k + 1
                hi, lo = weights(st, w_hi)[:, k, :], weights(st, w_lo)[:, k, :]
                pool.wait_ge(w_hi_ready.sem, w_hi_ready.at(b, n))
                G.tensor_tensor(lo, lo.bitcast(F32), hi.bitcast(F32), ALU.subtract).then_inc(w_ready.sem, 1)

            def rstd_of(b, st, t):
                if st not in LN_RANK:
                    return
                n = LN_RANK[st] * NT + t
                pool.wait_ge(ln_mv.sem, ln_mv.at(b, n + 1))
                G.tensor_scalar(var_eps[:, n % 3, :], mv[:, n % 3, 1:2], EPS, None, ALU.add).then_inc(ln_eps.sem, 1)
                pool.wait_ge(ln_eps.sem, ln_eps.at(b, n + 1))
                G.tensor_tensor(rstd[:, n % 3, :], var_eps[:, n % 3, :], minus_half[:, :], ALU.pow
                                ).then_inc(ln_rstd.sem, 1)

            def bias_x(b, st, t):
                if st not in BIAS_RANK:
                    return
                if st in LN_RANK:
                    pool.wait_ge(xn_ready.sem, xn_ready.at(b, LN_RANK[st] * NT + t + 1))
                else:
                    pool.wait_ge(x_new.sem, x_new.at(b, (UPD_RANK[st] - 1) * NT + t + 1))
                G.tensor_tensor(x[:, t, :], x[:, t, :], bx[st][:, :], ALU.add).then_inc(x_biased.sem, 1)

            def rope(b, st, t):
                a, s = ATT[st], qs[st]
                if not a.rope:
                    return
                n = a.qk_feats // 16
                pool.wait_ge(s["qkv"].sem, s["qkv"].at(b, t + 1))
                src = qkv[t % 3][:, 0:a.qk_feats]
                if t >= 1:
                    pool.wait_ge(s["roped"].sem, s["roped"].at(b, t))
                for im in range(2):
                    o = rs.rearrange("p (h d c) -> p h d c", d=8, c=2)[:, :, :, im]
                    i_ = src.rearrange("p (h d c) -> p h d c", d=8, c=2)[:, :, :, 1 - im]
                    sn = sin2[:, t, :].rearrange("p (d c) -> p d c", c=2)[:, :, im].unsqueeze(1).to_broadcast([P, n, 8])
                    last = G.tensor_tensor(o, i_, sn, ALU.mult)
                last.then_inc(s["sin"].sem, 1)

            def copy_v(b, st, t):
                a, s = ATT[st], qs[st]
                pool.wait_ge(s["qkv"].sem, s["qkv"].at(b, t + 1))
                v = values(a)
                if t == 0:
                    G.memset(v[:, :, :, a.dim:a.dim + 1], 1.0).then_inc(s["v_ones"].sem, 1)
                G.tensor_copy(v[:, t, :, 0:a.dim],
                              qkv[t % 3][:, a.qk_feats:a.feats].rearrange("p (h d) -> p h d", h=8)
                              ).then_inc(s["v"].sem, 1)

            def part3(b, st, t):
                a, s = ATT[st], qs[st]
                pool.wait_ge(s["p2"].sem, s["p2"].at(b, t + 1))
                G.tensor_tensor(parts[t % 3][:, 2, 0:a.qk_feats], rest[t % 2][:, 0:a.qk_feats],
                                parts[t % 3][:, 1, 0:a.qk_feats], ALU.subtract).then_inc(s["p3"].sem, 1)

            def chain(b, its):
                rstd_of(b, *its[0])
                rstd_of(b, *its[1])
                for i in range(len(its) + 7):
                    if i + 2 < len(its):
                        rstd_of(b, *its[i + 2])
                    if i < len(its):
                        st, t = its[i]
                        nb, nst = (b, st + 1) if st < MOE_B else (b + 1, FFN_A)
                        if nb < BATCH and 2 <= t < 2 + chunks_of[nst]:
                            split_chunk(nb, nst, t - 2)
                    if i < len(its):
                        bias_x(b, *its[i])
                    if 2 <= i < len(its) + 2 and its[i - 2][0] in ATT:
                        rope(b, *its[i - 2])
                        copy_v(b, *its[i - 2])
                    if 4 <= i < len(its) + 4 and its[i - 4][0] in ATT:
                        part3(b, *its[i - 4])

            def attention(b, st):
                a, s = ATT[st], qs[st]
                pool.wait_ge(s["partT"].sem, s["partT"].at(b, NT))
                for u in range(3):
                    _, k = q_and_k(a, aug_main(a, u))
                    last = G.memset(k[96:98, :, :, :], 1.0)
                last.then_inc(s["ones"].sem, 1)
                for g in range(a.units * len(a.steps)):
                    c, j, q0, w = a.steps[g % len(a.steps)]
                    if j < 4 * c:
                        continue
                    for pr in range(a.pairs):
                        e = g * a.pairs + pr
                        pool.wait_ge(s["exp"].sem, s["exp"].at(b, e + 1))
                        p = probs[:, e % 6, :, 0:P]
                        G.affine_select(out=p, in_=p, compare_op=ALU.is_ge, fill=0.0, base=0,
                                        pattern=[[0, 2], [1, P]], channel_multiplier=-1
                                        ).then_inc(s["masked"].sem, 1)

            pool.wait_ge(s_eff["router_parts"], 1)
            G.tensor_tensor(whl[:, 1, :, :], whl_raw, whl[:, 0, :, :].bitcast(F32), ALU.subtract
                            ).then_inc(s_eff["router_parts"], 1)
            for b in range(BATCH):
                chain(b, items[0])
                attention(b, QKV0)
                if b == 0:
                    pool.wait_ge(s_w, 16 * 4)
                    pool.wait_ge(s_eff["half_bias"], 1)
                chain(b, items[1])
                attention(b, QKV1)
                chain(b, items[2])


_INS = ["L0_attn_x", "L0_attn_w_qkv", "L0_attn_b_qkv", "L0_attn_w_o", "L0_attn_b_o", "L0_ffn_W", "L0_ffn_lora_A",
        "L0_ffn_lora_B", "L0_ffn_magnitude", "L1_attn_w_qkv", "L1_attn_b_qkv", "L1_attn_w_o", "L1_attn_b_o",
        "L1_ffn_W_base", "L1_ffn_b_base", "L1_ffn_W_router", "L1_ffn_lora_A", "L1_ffn_lora_B"]


def kernel(**inputs):
    import concourse.bacc as bacc
    from concourse.bass_utils import run_bass_kernel_spmd

    a = {n: np.asarray(inputs[n]) for n in _INS}
    lora_a = a["L1_ffn_lora_A"].reshape(ER, D)
    inv_freq = (1.0 / np.float32(10000.0) ** (np.arange(0, 16, 2, dtype=np.float32) / np.float32(16))).astype(np.float32)
    angle = np.arange(SEQ, dtype=np.float32)[:, None] * inv_freq[None, :]
    cos, sin = np.cos(angle).astype(np.float32), np.sin(angle).astype(np.float32)
    arrays = {
        "x": a["L0_attn_x"],
        "rope_cos": np.repeat(cos, 2, axis=1),
        "rope_sin": np.stack([-sin, sin], axis=-1).reshape(SEQ, 16),
        "ffn_w": a["L0_ffn_W"].T, "ffn_a": a["L0_ffn_lora_A"], "ffn_b": a["L0_ffn_lora_B"].T,
        "mag": a["L0_ffn_magnitude"],
        "wqkv0": a["L0_attn_w_qkv"].T[:, A0.feature_order()], "bqkv0": a["L0_attn_b_qkv"][A0.feature_order()],
        "wo0": a["L0_attn_w_o"].T, "bo0": a["L0_attn_b_o"],
        "wqkv1": a["L1_attn_w_qkv"].T[:, A1.feature_order()], "bqkv1": a["L1_attn_b_qkv"][A1.feature_order()],
        "wo1": a["L1_attn_w_o"].T, "bo1": a["L1_attn_b_o"],
        "base": a["L1_ffn_W_base"].T, "bbase": a["L1_ffn_b_base"],
        "hl": np.concatenate([lora_a, a["L1_ffn_W_router"]], axis=0).T,
        "lora_b": a["L1_ffn_lora_B"].transpose(0, 2, 1).reshape(ER, D),
    }
    arrays = {f"{n}_dram": np.ascontiguousarray(v) for n, v in arrays.items()}
    nc = bacc.Bacc("TRN2", target_bir_lowering=False, num_devices=1)
    w = {n[:-5]: nc.dram_tensor(n, v.shape, F32, kind="ExternalInput").ap() for n, v in arrays.items()}
    scratch = {n: nc.dram_tensor(f"staging_{n}", w[n].shape if n in w else (D, D), F32, kind="Internal").ap()
               for n in ("wqkv0", "wo0", "base", "wqkv1", "wo1", "dora")}
    out = nc.dram_tensor("out_dram", (BATCH, SEQ, D), F32, kind="ExternalOutput").ap()
    build(nc, w.pop("x"), w.pop("rope_cos"), w.pop("rope_sin"), w, scratch, out)
    r = run_bass_kernel_spmd(nc, [arrays], core_ids=[0])
    return r.results[0]["out_dram"]
```
